# Optimizing a Trainium2 kernel written in Bass

```python
import numpy as np
import jax
import jax.numpy as jnp

def _softmax(x, axis=-1):
    return jax.nn.softmax(x, axis=axis)

def _gelu(x):
    return jax.nn.gelu(x, approximate=True)

def _silu(x):
    return jax.nn.silu(x)

def _sigmoid(x):
    return jax.nn.sigmoid(x)

def _layernorm(x, axis=-1, eps=1e-05):
    m = jnp.mean(x, axis=axis, keepdims=True)
    v = jnp.var(x, axis=axis, keepdims=True)
    return (x - m) / jnp.sqrt(v + eps)

def _scatter_add(tgt, idx, src, axis=0):
    return tgt.at[idx].add(src)

def _segment_sum(src, seg, n):
    return jax.ops.segment_sum(src, seg, n)
kernel_name = 'mk_xattn_ffn_d2_seqx_r8_561429'

def setup_inputs(seed: int=0):
    np.random.seed(seed)
    _w = jnp.asarray

    def _rec_inputs():
        import jax
        import jax.numpy as jnp
        _rk = jax.random.key(seed)
        x = -0.0002928 + 1 * jax.random.normal(jax.random.fold_in(_rk, 1), (16, 256, 128), jnp.float32)
        _lenS = 256 - jax.random.randint(jax.random.fold_in(_rk, 7), (16,), 0, max(1, 256 // 4) + 1, jnp.int32)
        _lenS2 = 64 - jax.random.randint(jax.random.fold_in(_rk, 8), (16,), 0, max(1, 64 // 4) + 1, jnp.int32)
        _ctx_512P = jax.random.normal(jax.random.fold_in(_rk, 11), (16, 16, 64), jnp.float32)
        _ctx_512c = jax.random.dirichlet(jax.random.fold_in(_rk, 511), 0.3 * jnp.ones((16,), jnp.float32), (16, 64))
        _ctx_512t = jnp.einsum('bsk,bkd->bsd', _ctx_512c, _ctx_512P)
        _ctx_512t = _ctx_512t * jax.lax.rsqrt(jnp.mean(jnp.square(_ctx_512t)) + 1e-12) * 0.953939
        ctx_512 = 0.00222621 + 0.99962 * (_ctx_512t + 0.3 * jax.random.normal(jax.random.fold_in(_rk, 611), (16, 64, 64), jnp.float32))
        return (x, ctx_512)
    x, ctx_512 = _rec_inputs()

    def _L0_xattn_setup():
        import jax, jax.numpy as jnp
        import numpy as np
        B, T, TC, C, CC, H = (2, 256, 64, 128, 64, 16)
        D = C // H

        def _heads(t):
            b, l, _ = t.shape
            return t.reshape(b, l, H, D).transpose(0, 2, 1, 3)
        key = jax.random.key(seed)
        ks = jax.random.split(key, 18)
        w = lambda k, i, o: jax.random.normal(k, (i, o), jnp.float32) / np.sqrt(i).astype(np.float32)
        return {'x': jax.random.normal(ks[0], (B, T, C), jnp.float32), 'cross_input': jax.random.normal(ks[1], (B, TC, CC), jnp.float32), 'Wk': w(ks[2], C, C), 'bk': jnp.zeros((C,), jnp.float32), 'Wq': w(ks[3], C, C), 'bq': jnp.zeros((C,), jnp.float32), 'Wv': w(ks[4], C, C), 'bv': jnp.zeros((C,), jnp.float32), 'Wck': w(ks[5], CC, C), 'bck': jnp.zeros((C,), jnp.float32), 'Wcq': w(ks[6], C, C), 'bcq': jnp.zeros((C,), jnp.float32), 'Wcv': w(ks[7], CC, C), 'bcv': jnp.zeros((C,), jnp.float32), 'Wp': w(ks[8], C, C), 'bp': jnp.zeros((C,), jnp.float32)}
    _L0_xattn_all = _L0_xattn_setup()
    _L0_xattn_in = {k: v for k, v in _L0_xattn_all.items() if k in ('Wk', 'bk', 'Wq', 'bq', 'Wv', 'bv', 'Wck', 'bck', 'Wcq', 'bcq', 'Wcv', 'bcv', 'Wp', 'bp')}
    del _L0_xattn_all

    def _L0_ffn_setup():
        import jax, jax.numpy as jnp
        import numpy as np
        from jax import lax
        B, S, H = (2, 128, 128)
        I = 64
        E = 32
        TOP_K = 4
        N_GROUP = 4
        TOPK_GROUP = 2
        SCALE = 2.5
        N_SHARED = 2
        SH_I = I * N_SHARED

        def _route(tokens, router_weight, router_bias):
            logits = tokens.astype(jnp.float32) @ router_weight.astype(jnp.float32).T
            scores = jax.nn.sigmoid(logits)
            sfc = scores + router_bias[None, :]
            T = tokens.shape[0]
            grp = sfc.reshape(T, N_GROUP, E // N_GROUP)
            group_scores = lax.top_k(grp, 2)[0].sum(-1)
            _, gidx = lax.top_k(group_scores, TOPK_GROUP)
            gmask = jax.nn.one_hot(gidx, N_GROUP, dtype=sfc.dtype).sum(1)
            smask = jnp.broadcast_to(gmask[:, :, None], (T, N_GROUP, E // N_GROUP)).reshape(T, E)
            tmp = jnp.where(smask > 0, sfc, 0.0)
            _, topk_idx = lax.top_k(tmp, TOP_K)
            topk_w = jnp.take_along_axis(scores, topk_idx, axis=1)
            topk_w = topk_w / (topk_w.sum(-1, keepdims=True) + 1e-20)
            topk_w = topk_w * SCALE
            return (topk_idx, topk_w)
        key = jax.random.key(seed)
        ks = jax.random.split(key, 10)
        std = 0.02
        return {'hidden_states': jax.random.normal(ks[0], (B, S, H), jnp.float32), 'router_weight': jax.random.normal(ks[1], (E, H), jnp.float32) * std, 'router_bias': jnp.zeros((E,), jnp.float32), 'gate_w': jax.random.normal(ks[2], (E, I, H), jnp.float32) * std, 'up_w': jax.random.normal(ks[3], (E, I, H), jnp.float32) * std, 'down_w': jax.random.normal(ks[4], (E, H, I), jnp.float32) * std, 'shared_gate_w': jax.random.normal(ks[5], (SH_I, H), jnp.float32) * std, 'shared_up_w': jax.random.normal(ks[6], (SH_I, H), jnp.float32) * std, 'shared_down_w': jax.random.normal(ks[7], (H, SH_I), jnp.float32) * std}
    _L0_ffn_all = _L0_ffn_setup()
    _L0_ffn_in = {k: v for k, v in _L0_ffn_all.items() if k in ('router_weight', 'router_bias', 'gate_w', 'up_w', 'down_w', 'shared_gate_w', 'shared_up_w', 'shared_down_w')}
    del _L0_ffn_all

    def _L1_xattn_setup():
        import jax, jax.numpy as jnp
        import numpy as np
        DIM = 128
        LATENT_DIM = 64
        NUM_HEADS = 16
        HEAD_DIM = DIM // NUM_HEADS
        SCALE = HEAD_DIM ** (-0.5)
        key = jax.random.key(seed)
        k1, k2, k3, k4, k5 = jax.random.split(key, 5)
        B, xN, zN = (2, 256, 256)
        x = jax.random.normal(k1, (B, xN, DIM), dtype=jnp.float32)
        z = jax.random.normal(k2, (B, zN, LATENT_DIM), dtype=jnp.float32)
        Wq = jax.random.normal(k3, (DIM, DIM), dtype=jnp.float32) * DIM ** (-0.5)
        Wkv = jax.random.normal(k4, (2 * DIM, LATENT_DIM), dtype=jnp.float32) * LATENT_DIM ** (-0.5)
        Wo = jax.random.normal(k5, (DIM, DIM), dtype=jnp.float32) * DIM ** (-0.5)
        return {'x': x, 'z': z, 'Wq': Wq, 'Wkv': Wkv, 'Wo': Wo}
    _L1_xattn_all = _L1_xattn_setup()
    _L1_xattn_in = {k: v for k, v in _L1_xattn_all.items() if k in ('Wq', 'Wkv', 'Wo')}
    del _L1_xattn_all

    def _L1_ffn_setup():
        import jax, jax.numpy as jnp
        import numpy as np
        TOP_K = 2
        key = jax.random.key(seed)
        k1, k2, k3, k4 = jax.random.split(key, 4)
        B, S, H, I, E = (2, 256, 128, 512, 8)
        return {'hidden_states': jax.random.normal(k1, (B, S, H), jnp.float32), 'gate_w': jax.random.normal(k2, (E, H), jnp.float32) * 0.02, 'gate_up_proj': jax.random.normal(k3, (E, 2 * I, H), jnp.float32) * 0.02, 'down_proj': jax.random.normal(k4, (E, H, I), jnp.float32) * 0.02}
    _L1_ffn_all = _L1_ffn_setup()
    _L1_ffn_in = {k: v for k, v in _L1_ffn_all.items() if k in ('gate_w', 'gate_up_proj', 'down_proj')}
    del _L1_ffn_all
    return {'x': x, 'ctx_512': ctx_512, 'L0_xattn_Wk': _L0_xattn_in['Wk'], 'L0_xattn_bk': _L0_xattn_in['bk'], 'L0_xattn_Wq': _L0_xattn_in['Wq'], 'L0_xattn_bq': _L0_xattn_in['bq'], 'L0_xattn_Wv': _L0_xattn_in['Wv'], 'L0_xattn_bv': _L0_xattn_in['bv'], 'L0_xattn_Wck': _L0_xattn_in['Wck'], 'L0_xattn_bck': _L0_xattn_in['bck'], 'L0_xattn_Wcq': _L0_xattn_in['Wcq'], 'L0_xattn_bcq': _L0_xattn_in['bcq'], 'L0_xattn_Wcv': _L0_xattn_in['Wcv'], 'L0_xattn_bcv': _L0_xattn_in['bcv'], 'L0_xattn_Wp': _L0_xattn_in['Wp'], 'L0_xattn_bp': _L0_xattn_in['bp'], 'L0_ffn_router_weight': _L0_ffn_in['router_weight'], 'L0_ffn_router_bias': _L0_ffn_in['router_bias'], 'L0_ffn_gate_w': _L0_ffn_in['gate_w'], 'L0_ffn_up_w': _L0_ffn_in['up_w'], 'L0_ffn_down_w': _L0_ffn_in['down_w'], 'L0_ffn_shared_gate_w': _L0_ffn_in['shared_gate_w'], 'L0_ffn_shared_up_w': _L0_ffn_in['shared_up_w'], 'L0_ffn_shared_down_w': _L0_ffn_in['shared_down_w'], 'L1_xattn_Wq': _L1_xattn_in['Wq'], 'L1_xattn_Wkv': _L1_xattn_in['Wkv'], 'L1_xattn_Wo': _L1_xattn_in['Wo'], 'L1_ffn_gate_w': _L1_ffn_in['gate_w'], 'L1_ffn_gate_up_proj': _L1_ffn_in['gate_up_proj'], 'L1_ffn_down_proj': _L1_ffn_in['down_proj']}

def reference(x, ctx_512, L0_xattn_Wk, L0_xattn_bk, L0_xattn_Wq, L0_xattn_bq, L0_xattn_Wv, L0_xattn_bv, L0_xattn_Wck, L0_xattn_bck, L0_xattn_Wcq, L0_xattn_bcq, L0_xattn_Wcv, L0_xattn_bcv, L0_xattn_Wp, L0_xattn_bp, L0_ffn_router_weight, L0_ffn_router_bias, L0_ffn_gate_w, L0_ffn_up_w, L0_ffn_down_w, L0_ffn_shared_gate_w, L0_ffn_shared_up_w, L0_ffn_shared_down_w, L1_xattn_Wq, L1_xattn_Wkv, L1_xattn_Wo, L1_ffn_gate_w, L1_ffn_gate_up_proj, L1_ffn_down_proj):
    import jax
    import jax.numpy as jnp

    def _L0_xattn_ref(x, cross_input, Wk, bk, Wq, bq, Wv, bv, Wck, bck, Wcq, bcq, Wcv, bcv, Wp, bp):
        import jax, jax.numpy as jnp
        import numpy as np
        B, T, TC, C, CC, H = (2, 256, 64, 128, 64, 16)
        D = C // H

        def _heads(t):
            b, l, _ = t.shape
            return t.reshape(b, l, H, D).transpose(0, 2, 1, 3)
        scale = np.float32(1.0 / np.sqrt(D))
        q = _heads(x @ Wq + bq)
        k = _heads(x @ Wk + bk)
        v = _heads(x @ Wv + bv)
        att = jnp.einsum('bhqd,bhkd->bhqk', q, k) * scale
        causal = jnp.tril(jnp.ones((T, T), bool))
        att = jnp.where(causal[None, None], att, -jnp.inf)
        y = jnp.einsum('bhqk,bhkd->bhqd', jax.nn.softmax(att, axis=-1), v)
        qc = _heads(x @ Wcq + bcq)
        kc = _heads(cross_input @ Wck + bck)
        vc = _heads(cross_input @ Wcv + bcv)
        attc = jnp.einsum('bhqd,bhkd->bhqk', qc, kc) * scale
        y = y + jnp.einsum('bhqk,bhkd->bhqd', jax.nn.softmax(attc, axis=-1), vc)
        y = y.transpose(0, 2, 1, 3).reshape(x.shape[0], T, C)
        return y @ Wp + bp

    def _L0_ffn_ref(hidden_states, router_weight, router_bias, gate_w, up_w, down_w, shared_gate_w, shared_up_w, shared_down_w):
        import jax, jax.numpy as jnp
        import numpy as np
        from jax import lax
        B, S, H = (2, 128, 128)
        I = 64
        E = 32
        TOP_K = 4
        N_GROUP = 4
        TOPK_GROUP = 2
        SCALE = 2.5
        N_SHARED = 2
        SH_I = I * N_SHARED

        def _route(tokens, router_weight, router_bias):
            logits = tokens.astype(jnp.float32) @ router_weight.astype(jnp.float32).T
            scores = jax.nn.sigmoid(logits)
            sfc = scores + router_bias[None, :]
            T = tokens.shape[0]
            grp = sfc.reshape(T, N_GROUP, E // N_GROUP)
            group_scores = lax.top_k(grp, 2)[0].sum(-1)
            _, gidx = lax.top_k(group_scores, TOPK_GROUP)
            gmask = jax.nn.one_hot(gidx, N_GROUP, dtype=sfc.dtype).sum(1)
            smask = jnp.broadcast_to(gmask[:, :, None], (T, N_GROUP, E // N_GROUP)).reshape(T, E)
            tmp = jnp.where(smask > 0, sfc, 0.0)
            _, topk_idx = lax.top_k(tmp, TOP_K)
            topk_w = jnp.take_along_axis(scores, topk_idx, axis=1)
            topk_w = topk_w / (topk_w.sum(-1, keepdims=True) + 1e-20)
            topk_w = topk_w * SCALE
            return (topk_idx, topk_w)
        tokens = hidden_states.reshape(-1, H)
        topk_idx, topk_w = _route(tokens, router_weight, router_bias)
        gate_vals = jax.nn.silu(jnp.einsum('th,eih->tei', tokens, gate_w))
        up_vals = jnp.einsum('th,eih->tei', tokens, up_w)
        hidden_vals = gate_vals * up_vals
        expert_out = jnp.einsum('tei,ehi->teh', hidden_vals, down_w)
        sel = jnp.take_along_axis(expert_out, topk_idx[:, :, None], axis=1)
        mixed = (sel * topk_w[:, :, None].astype(sel.dtype)).sum(1)
        mixed = mixed.reshape(hidden_states.shape)
        sg = jax.nn.silu(jnp.einsum('bsh,ih->bsi', hidden_states, shared_gate_w))
        su = jnp.einsum('bsh,ih->bsi', hidden_states, shared_up_w)
        shared = jnp.einsum('bsi,hi->bsh', sg * su, shared_down_w)
        return mixed + shared

    def _L1_xattn_ref(x, z, Wq, Wkv, Wo):
        import jax, jax.numpy as jnp
        import numpy as np
        DIM = 128
        LATENT_DIM = 64
        NUM_HEADS = 16
        HEAD_DIM = DIM // NUM_HEADS
        SCALE = HEAD_DIM ** (-0.5)
        B, xN, _ = x.shape
        _, zN, _ = z.shape
        Q = (x @ Wq.T).reshape(B, xN, NUM_HEADS, HEAD_DIM)
        KV = (z @ Wkv.T).reshape(B, zN, 2, NUM_HEADS, HEAD_DIM)
        K = KV[:, :, 0]
        V = KV[:, :, 1]
        attn = jnp.einsum('bqhd,bkhd->bhqk', Q, K) * SCALE
        attn = jax.nn.softmax(attn, axis=-1)
        O = jnp.einsum('bhqk,bkhd->bqhd', attn, V).reshape(B, xN, DIM)
        return O @ Wo.T

    def _L1_ffn_ref(hidden_states, gate_w, gate_up_proj, down_proj):
        import jax, jax.numpy as jnp
        import numpy as np
        TOP_K = 2
        B, S, H = hidden_states.shape
        E = gate_w.shape[0]
        x = hidden_states.reshape(-1, H)
        T = x.shape[0]
        probs = jax.nn.softmax(x @ gate_w.T, axis=-1)
        w, idx = jax.lax.top_k(probs, TOP_K)
        w = w / jnp.sum(w, axis=-1, keepdims=True)
        combine = jnp.zeros((T, E), x.dtype).at[jnp.arange(T)[:, None], idx].add(w)

        def step(acc, inputs):
            gup, dn, ce = inputs
            g, u = jnp.split(x @ gup.T, 2, axis=-1)
            acc = acc + ce[:, None] * (jax.nn.silu(g) * u @ dn.T)
            return (acc, None)
        out, _ = jax.lax.scan(step, jnp.zeros_like(x), (gate_up_proj, down_proj, combine.T))
        return out.reshape(B, S, H)
    x = x + _L0_xattn_ref(_layernorm(x, axis=-1), ctx_512, L0_xattn_Wk, L0_xattn_bk, L0_xattn_Wq, L0_xattn_bq, L0_xattn_Wv, L0_xattn_bv, L0_xattn_Wck, L0_xattn_bck, L0_xattn_Wcq, L0_xattn_bcq, L0_xattn_Wcv, L0_xattn_bcv, L0_xattn_Wp, L0_xattn_bp)
    x = x + _L0_ffn_ref(_layernorm(x, axis=-1), L0_ffn_router_weight, L0_ffn_router_bias, L0_ffn_gate_w, L0_ffn_up_w, L0_ffn_down_w, L0_ffn_shared_gate_w, L0_ffn_shared_up_w, L0_ffn_shared_down_w)
    x = x + _L1_xattn_ref(_layernorm(x, axis=-1), ctx_512, L1_xattn_Wq, L1_xattn_Wkv, L1_xattn_Wo)
    x = x + _L1_ffn_ref(_layernorm(x, axis=-1), L1_ffn_gate_w, L1_ffn_gate_up_proj, L1_ffn_down_proj)
    return x

_drawn_inputs = setup_inputs


def setup_inputs(seed=0):
    import zlib

    import numpy as np

    out = dict(_drawn_inputs(seed))
    spreads = {'L0_xattn_bk': (0.0, 0.8),
     'L0_xattn_bq': (0.0, 0.501),
     'L0_xattn_bv': (0.0, 0.1),
     'L0_xattn_bck': (0.0, 0.8),
     'L0_xattn_bcq': (0.0, 0.406),
     'L0_xattn_bcv': (0.0, 0.1),
     'L0_xattn_bp': (0.0, 0.1),
     'L0_ffn_router_bias': (0.0, 0.8)}
    factors = {'L0_ffn_router_weight': 8.0,
     'L0_ffn_gate_w': 8.0,
     'L0_ffn_up_w': 8.0,
     'L0_ffn_down_w': 8.0,
     'L0_ffn_shared_gate_w': 8.0,
     'L0_ffn_shared_up_w': 8.0,
     'L0_ffn_shared_down_w': 8.0,
     'L1_ffn_gate_w': 8.0,
     'L1_ffn_gate_up_proj': 8.0,
     'L1_ffn_down_proj': 8.0}
    for name, (base, spread) in spreads.items():
        noise = np.random.default_rng([zlib.crc32(name.encode()), seed]).standard_normal(out[name].shape)
        drawn = base * np.exp(spread * noise) if base else spread * noise
        out[name] = jnp.asarray(drawn.astype(out[name].dtype))
    for name, factor in factors.items():
        out[name] = (out[name] * factor).astype(out[name].dtype)
    return out
```

```python
from contextlib import ExitStack

import numpy as np

import concourse.bass as bass
from concourse import mybir

F32 = mybir.dt.float32
BF = mybir.dt.bfloat16
ALU = mybir.AluOpType
ACT = mybir.ActivationFunctionType
AX = mybir.AxisListType

P = 128
B, T, C = 16, 256, 128
TC, CC = 64, 64
H, D = 16, 8
NJ = H // 2
NT = B * T // P
NCTX = B * TC
SCALE = float(np.float32(1.0 / np.sqrt(D)))
EPS = 1e-5
SLOTS = 6
SROWS = SLOTS * 16
MROWS = 6
MASKED = -1e38
HUGE = 3e38
E0, I0, K0, G0 = 32, 64, 4, 4
ROUTE_SCALE = 2.5
E1, I1, K1 = 8, 512, 2
CH = 512
NCH = B * T // CH
CT = CH // P
U0 = E0 * I0 // P + 1
U1 = E1 * I1 // P


class Layer:

    def __init__(self, own, order):
        self.own = own
        self.order = order
        self.kinds = 2 if own else 1
        self.tw = T * self.kinds
        self.qc = T if own else 0
        self.units = NJ if own else NJ // 2
        self.uses = [e for e in order if e in ("XT", "Q", "KV", "M", "Y0", "Y1", "Y2", "YT", "O")]

        self.total = self.before(B + 2, "O") + 1

    def live(self, e, prep, nat, trans, tail):
        if e in ("XT", "Q"):
            return prep
        if e == "KV":
            return prep or nat
        if e[0] in "NM":
            return nat
        if e in ("Y1", "Y2", "YT", "O"):
            return tail
        return trans

    def before(self, s, e):
        count = 0
        if isinstance(s, int):
            parts = lambda t: (t < B, 0 <= t - 1 < B, 0 <= t - 2 < B, 0 <= t - 3 < B)
            for t in range(s):
                count += sum(self.live(u, *parts(t)) for u in self.uses)
            for u in self.uses:
                if u == e:
                    return count
                count += self.live(u, *parts(s))
        three = self.before(3, self.uses[0])
        return (s - 3) * len(self.uses) + (three + self.uses.index(e))


F_USES = 4 * NCH
CONSTS = 16 * 16
SET_UP = 29
ROUTING = ([("XT", 2, 3), ("R", 4, 4), ("W", 13, 5)], [("XT", 3, 3), ("R", 6, 4), ("W", 24, 5)])
LN_AT, Y_AT = 0, 1
ROUTE_PARTS = 8
ROUTE_LINKS = (23, 15)

LAYERS = [
    Layer(True, ["Y1", "XT", "Y2", "T0", "Q", "N0", "T1", "P0", "KV", "N1", "T2", "P1", "N2", "T3", "P2", "N3", "T4", "P3", "N4", "Y0", "T5", "P4", "N5", "N6", "T6", "P5", "N7", "T7", "P6", "M", "P7", "YT", "O"]),
    Layer(False, ["Y2", "XT", "YT", "Q", "O", "T0", "N0", "T1", "P0", "N1", "T2", "P1", "N2", "N3", "T3", "P2", "P3", "M"]),
]


class AttentionSignals:

    def __init__(self, sem, l):
        self.mv_ready = sem(f"mv_ready{l}")
        self.rstd_chain = sem(f"rstd_chain{l}")
        self.rstd_ready = sem(f"rstd_ready{l}")
        self.ln_chain = sem(f"ln_chain{l}")
        self.xn_ready = sem(f"xn_ready{l}")
        self.misc_full = sem(f"misc_full{l}")
        self.misc_free = sem(f"misc_free{l}")
        self.cut_chain = sem(f"cut_chain{l}")
        self.q_cut = sem(f"q_cut{l}")
        self.k_cut = sem(f"k_cut{l}")
        self.stack_written = sem(f"stack_written{l}")
        self.stack_in = sem(f"stack_in{l}")
        self.m_written = sem(f"m_written{l}")
        self.m_in = sem(f"m_in{l}")
        self.nat_full = [sem(f"nat_full{l}_{k}") for k in range(2)]
        self.nat_free = [sem(f"nat_free{l}_{k}") for k in range(2)]
        self.tr_full = [sem(f"tr_full{l}_{k}") for k in range(2)]
        self.probs = [sem(f"probs{l}_{k}") for k in range(2)]
        self.m_chain = sem(f"m_chain{l}")
        self.m_cut = sem(f"m_cut{l}")
        self.pv_done = sem(f"pv_done{l}")
        self.yu_ready = sem(f"yu_ready{l}")
        self.vx_ready = sem(f"vx_ready{l}")
        self.xb_ready = sem(f"xb_ready{l}")
        self.y_chain = sem(f"y_chain{l}")
        self.y_ready = sem(f"y_ready{l}")


class ExpertSignals:

    def __init__(self, sem, l):
        self.mv_ready = sem(f"f_mv_ready{l}")
        self.rstd_chain = sem(f"f_rstd_chain{l}")
        self.rstd_ready = sem(f"f_rstd_ready{l}")
        self.ln_chain = sem(f"f_ln_chain{l}")
        self.xn_ready = sem(f"f_xn_ready{l}")
        self.misc_full = sem(f"f_misc_full{l}")
        self.misc_free = sem(f"f_misc_free{l}")
        self.wt_zeroed = sem(f"f_wt_zeroed{l}")
        self.ex_ready = sem(f"f_ex_ready{l}")
        self.r_chain = sem(f"f_r_chain{l}")
        self.w_cut = sem(f"f_w_cut{l}")
        self.gate_full = sem(f"f_gate_full{l}")
        self.up_full = sem(f"f_up_full{l}")
        self.wb_full = sem(f"f_wb_full{l}")
        self.s_ready = sem(f"f_s_ready{l}")
        self.t_ready = sem(f"f_t_ready{l}")
        self.xw_ready = sem(f"f_xw_ready{l}")
        self.h_ready = sem(f"f_h_ready{l}")
        self.h_used = sem(f"f_h_used{l}")
        self.yt_ready = sem(f"f_yt_ready{l}")


def at_least(eng, sem, value):
    if isinstance(value, int) and value <= 0:
        return
    eng.wait_ge(sem, value)


def steps(eng, step):
    for s in range(4):
        step(s, s % 2, s < B, 0 <= s - 1 < B, 0 <= s - 2 < B, 0 <= s - 3 < B)
    with eng.Fori(0, (B - 4) // 2) as g:
        for k in range(2):
            step(g * 2 + (4 + k), k, True, True, True, True)
    for s in (B, B + 1, B + 2):
        step(s, s % 2, False, s - 1 < B, s - 2 < B, True)


def chunks(eng, chunk):
    chunk(0, 0, True)
    with eng.Fori(0, (NCH - 2) // 2) as g:
        for k in range(2):
            chunk(g * 2 + (1 + k), (1 + k) % 2, True)
    chunk(NCH - 1, (NCH - 1) % 2, False)


def bass_two_layers(nc, t, out):
    ctx = ExitStack()
    with ctx:
        def sb(name, shape, dt=F32):
            return ctx.enter_context(nc.sbuf_tensor(name, shape, dt))

        def sem(name):
            return ctx.enter_context(nc.semaphore(name))

        identf, identb = sb("identf", [P, P]), sb("identb", [P, P], BF)
        mask_nat, mask_tr = sb("mask_nat", [P, 2, P], BF), sb("mask_tr", [P, 2, P], BF)
        keep = sb("keep", [P, 2])
        lower = sb("lower", [P, G0, G0])
        sel0 = sb("sel0", [P, U0 - 1, P], BF)
        sel1 = sb("sel1", [P, E1, P], BF)
        bias_in = sb("bias_in", [P, 8])
        bias_kz = sb("bias_kz", [P, 2, 2])
        bias_y = sb("bias_y", [P, 2])
        bp_row = sb("bp_row", [P, P])
        w_att = [sb("w_att0", [P, 5, P]), sb("w_att1", [P, 2, P])]
        w_ctx = sb("w_ctx", [CC, 2, 2, P])
        neg_half = sb("neg_half", [P, CT])
        w_router0, w_router1 = sb("w_router0", [P, E0]), sb("w_router1", [P, E1])
        router_bias = sb("router_bias", [P, E0])
        w_gate0, w_up0 = (sb(n, [P, U0, P]) for n in ("w_gate0", "w_up0"))

        X = sb("X", [P, NT, C])
        KC = sb("KC", [P, NJ, 2 * NCTX], BF)
        kc_sides = KC[:, :, :].rearrange("p j (b s t) -> p (j b) s t", s=2, t=TC)
        region4 = sb("region4", [P, U0 * P])
        VC = [region4[:, 0:B * P].rearrange("p (b c) -> p b c", b=B), sb("VC1", [P, B, P])]
        w_down0 = region4[:, :].rearrange("p (u c) -> p u c", u=U0)

        region1 = sb("region1", [P, 12288])
        KZ = [region1[:, 2048 * k:2048 * (k + 1)].bitcast(BF).rearrange("p (j s t) -> p j s t", j=NJ, s=2)
              for k in range(2)]
        ctx_t = region1[:, 4096:5120]
        kc_f = region1[:, 5120:7168]
        kc_r = region1[:, 7168:9216]
        kc_parts = region1[:, 9216:12288].bitcast(BF).rearrange("p (r n) -> p r n", r=3)
        w_gu1 = region1[:, 0:8192].rearrange("p (e a i n) -> p e a i n", e=E1, a=2, i=4)
        w_dn1 = region1[:, 8192:12288].rearrange("p (u n) -> p u n", u=U1)

        region2 = sb("region2", [P, 6656])
        QS = [region2[:, 2048 * k:2048 * (k + 1)].bitcast(BF) for k in range(2)]
        zeros_m = region2[0:MROWS, 4096:6144].bitcast(BF)
        PR = region2[:, 4096:6144].rearrange("p (r k n) -> p r k n", r=2, k=2)
        hid_s = region2[:, 0:1024].rearrange("p (r n) -> p r n", r=2)
        hid_t = region2[:, 1024:2048].rearrange("p (r n) -> p r n", r=2)
        hid_h = region2[:, 2048:3072].rearrange("p (r n) -> p r n", r=2)
        xw = region2[:, 3072:4096].rearrange("p (r n) -> p r n", r=2)
        xt_f = region2[:, 4096:5120].rearrange("p (r n) -> p r n", r=2)
        yt_f = region2[:, 5120:5632]
        wt_f = [region2[:, 5632 + 256 * k:5888 + 256 * k].bitcast(BF) for k in range(2)]
        xn_f = region2[:, 6144:6656].rearrange("p (t n) -> p t n", t=CT)

        stats = sb("stats", [P, CT, 6])
        mv = sb("mv", [P, CT, 2])
        var_e, rstd = sb("var_e", [P, CT]), sb("rstd", [P, CT])
        xn = sb("xn", [P, 2, C])
        xt = [sb(f"xt{k}", [P, T]) for k in range(2)]
        qf, kf, rest = (sb(n, [P, 2 * T]) for n in ("qf", "kf", "rest"))
        q_parts, k_parts = sb("q_parts", [P, 3, 2 * T], BF), sb("k_parts", [P, 3, 2 * T], BF)
        region3 = sb("region3", [P, 2048])
        V = [region3[:, 1024 * k:1024 * k + 1024].rearrange("p (k h n) -> p k h n", k=2, n=32) for k in range(2)]
        VX = [sb(f"VX{k}", [P, NJ, 32]) for k in range(2)]
        nmax, nmax_r = sb("nmax", [P, 4, 2, NJ]), sb("nmax_r", [P, 4, 2, NJ])
        nmax_p = sb("nmax_p", [P, 4, 2, 3, NJ], BF)
        mt = sb("mt", [48, 2 * T], BF)
        yu = sb("yu", [P, 2 * T])
        den = sb("den", [P, 32])
        y_own, y_ctx, y_all = sb("y_own", [P, 2, P]), sb("y_ctx", [P, 2, P]), sb("y_all", [P, 2, P])
        yt = sb("yt", [P, T])
        xb = sb("xb", [P, 2, C])

        ex, sig, biased, wsel, wgt, wrest, top_g = (
            region3[:, 128 * k:128 * k + 128].rearrange("p (t e) -> p t e", e=E0 if k < 6 else 8) for k in range(7))
        w_parts = region3[:, 896:1088].bitcast(BF).rearrange("p (t e) -> p t e", t=CT)
        gs = sb("gs", [P, CT, G0])
        cmp_a, cmp_b = sb("cmp_a", [P, CT, G0, G0]), sb("cmp_b", [P, CT, G0, G0])
        rank, gmask = sb("rank", [P, CT, G0]), sb("gmask", [P, CT, G0])
        cand0, mark0 = sb("cand0", [P, CT, E0 + 8 - K0]), sb("mark0", [P, CT, E0 + 8 - K0])
        cand1, mark1 = sb("cand1", [P, CT, E1 + 8 - K1]), sb("mark1", [P, CT, E1 + 8 - K1])
        top, take0, take1 = sb("top", [P, CT, 8]), sb("take0", [P, CT, 8]), sb("take1", [P, CT, 8])
        wsum, winv = sb("wsum", [P, CT]), sb("winv", [P, CT])

        bank = [ctx.enter_context(nc.psum_tensor(f"bank{i}", [P, 512], F32)) for i in range(8)]
        nat_ps, tr_ps, pv_ps, misc = bank[0:2], bank[2:4], bank[4:7], bank[7]
        gate_ps, up_ps, wb_ps, y_ps = bank[0:2], bank[2:4], bank[4:6], bank[6]

        q_scr = [[nc.dram_tensor(f"q_scr{l}_{k}", [SROWS + MROWS, NJ * LAYERS[l].tw], BF).ap() for k in range(2)]
                 for l in range(2)]
        k_scr = [nc.dram_tensor(f"k_scr{k}", [SROWS, NJ * 2 * T], BF).ap() for k in range(2)]
        kc_scr = [nc.dram_tensor(f"kc_scr{k}", [SROWS, NJ * 2 * NCTX], BF).ap() for k in range(2)]
        m_scr = [nc.dram_tensor(f"m_scr{l}", [MROWS, NJ * LAYERS[l].tw], BF).ap() for l in range(2)]

        consts_in, x_in, gu0_in, w1_in = sem("consts_in"), sem("x_in"), sem("gu0_in"), sem("w1_in")
        ctx_in = sem("ctx_in")
        set_up, bias_done, zeros_ready, scr_zeroed = (
            sem("set_up"), sem("bias_done"), sem("zeros_ready"), sem("scr_zeroed"))
        kc_full, kc_flat, kc_chain, kc_cut, kc_written, kc_in = (
            sem(n) for n in ("kc_full", "kc_flat", "kc_chain", "kc_cut", "kc_written", "kc_in"))
        vc_full, vc_free = sem("vc_full"), sem("vc_free")
        out_done, apart, stacks_zeroed = sem("out_done"), sem("apart"), sem("stacks_zeroed")

        A = [AttentionSignals(sem, l) for l in range(2)]
        F = [ExpertSignals(sem, l) for l in range(2)]

        def wait_alone(eng, sem, value):
            if isinstance(value, int):
                at_least(eng, sem, value)
                return
            eng.wait_ge(sem, value)
            eng.sem_inc(apart, 1)

        def stack_in_cols(buf, tw):
            return buf[:, 0:NJ * tw].rearrange("p (j t) -> p j t", j=NJ)

        block = ctx.enter_context(nc.Block())

        @block.sync
        def _(sp):
            n = 0
            for dst, name in ((identf[:, :], "c_identf"), (identb[:, :], "c_identb"), (keep[:, :], "c_keep"),
                              (mask_nat[:, :, :], "c_mask_nat"), (mask_tr[:, :, :], "c_mask_tr"),
                              (lower[:, :, :], "c_lower"), (sel0[:, :, :], "c_sel0"), (sel1[:, :, :], "c_sel1"),
                              (bias_in[:, 0:6], "biases"), (w_att[0][:, :, :], "w_att0"),
                              (w_att[1][:, :, :], "w_att1"), (w_ctx[:, :, :, :], "w_ctx"),
                              (w_router0[:, :], "w_router0"), (w_router1[:, :], "w_router1")):
                sp.dma_start(dst, t[name]).then_inc(consts_in, 16)
            sp.dma_start(bp_row[:, :], t["bp"].partition_broadcast(P)).then_inc(consts_in, 16)
            sp.dma_start(router_bias[:, :], t["router_bias"].partition_broadcast(P)).then_inc(consts_in, 16)
            sp.dma_start(ctx_t[0:CC, :], t["ctx"]).then_inc(ctx_in, 16)
            sp.dma_start(X[:, :, :], t["x"]).then_inc(x_in, 16)
            sp.dma_start(w_gate0[:, :, :], t["w_gate0"]).then_inc(gu0_in, 16)
            sp.dma_start(w_up0[:, :, :], t["w_up0"]).then_inc(gu0_in, 16)
            sp.wait_ge(zeros_ready, 1)
            for l in range(2):
                for k in range(2):
                    sp.dma_start(q_scr[l][k][SROWS:SROWS + MROWS, :], zeros_m[:, 0:NJ * LAYERS[l].tw])\
                      .then_inc(scr_zeroed, 16)
            for l in range(2):
                sp.wait_ge(kc_cut, l + 1)
                rows = kc_scr[l].rearrange("(r q) (j n) -> (q j) r n", r=SLOTS, j=NJ)
                for a, b, k in ((0, 3, 3), (3, 5, 2), (5, 6, 1)):
                    sp.dma_start(rows[:, a:b, :], kc_parts[:, 0:k, :]).then_inc(kc_written, 16)
            for l in range(2):
                lay, a = LAYERS[l], A[l]
                tw = lay.tw
                if l == 0:
                    sp.wait_ge(kc_written, 96)
                else:
                    sp.wait_ge(A[0].misc_free, LAYERS[0].total)
                    sp.dma_start(w_down0, t["w_down0"]).then_inc(gu0_in, 16)
                sp.dma_start(KC[0:SROWS, :, :].rearrange("p j n -> p (j n)"), kc_scr[l]).then_inc(kc_in, 16)
                if l == 0:
                    sp.wait_ge(scr_zeroed, 64)
                if l == 1:
                    sp.dma_start(w_gu1, t["w_gu1"]).then_inc(w1_in, 16)
                    sp.dma_start(w_dn1, t["w_dn1"]).then_inc(w1_in, 16)
                    sp.wait_ge(F[0].misc_free, F_USES)
                    sp.wait_ge(stacks_zeroed, 2)
                per_w = 96 if lay.own else 48
                per_r = 32 if lay.own else 16

                def step(s, par, prep, nat, trans, tail):
                    if prep:
                        wait_alone(sp, a.stack_in, (s - 1) * per_r)
                        wait_alone(sp, a.q_cut, s + 1)
                        rows = q_scr[l][par][0:SROWS, :].rearrange("(r q) (j n) -> (q j) r n", r=SLOTS, j=NJ)
                        for lo, hi, k in ((0, 3, 0), (3, 5, 1), (5, 6, 2)):
                            src = q_parts[:, k:k + 1, 0:tw].broadcast_to([P, hi - lo, tw])
                            sp.dma_start(rows[:, lo:hi, :], src).then_inc(a.stack_written, 16)
                        if lay.own:
                            wait_alone(sp, a.k_cut, s + 1)
                            rows = k_scr[par].rearrange("(r q) (j n) -> (q j) r n", r=SLOTS, j=NJ)
                            for lo, hi, k in ((0, 3, 3), (3, 5, 2), (5, 6, 1)):
                                sp.dma_start(rows[:, lo:hi, :], k_parts[:, 0:k, :]).then_inc(a.stack_written, 16)
                    def stacks_in():
                        wait_alone(sp, a.stack_written, (s + 1) * per_w)
                        for full in a.tr_full:
                            wait_alone(sp, full, (s - 1) * (lay.units if lay.own else lay.units // 2))
                        sp.dma_start(QS[par][0:SROWS + MROWS, 0:NJ * tw], q_scr[l][par])\
                          .then_inc(a.stack_in, 16)
                        if lay.own:
                            sp.dma_start(KZ[par][0:SROWS, :, :, :].rearrange("p j s t -> p (j s t)"), k_scr[par])\
                              .then_inc(a.stack_in, 16)

                    if nat:
                        wait_alone(sp, a.misc_free, lay.before(s, "M") + 1)
                        wait_alone(sp, a.m_in, (s - 1) * 16)
                        rows = m_scr[l].rearrange("m (j n) -> (m j) n", j=NJ)
                        sp.dma_start(rows, mt[:, 0:tw]).then_inc(a.m_written, 16)
                        wait_alone(sp, a.m_written, s * 16)
                        sp.dma_start(QS[1 - par][SROWS:SROWS + MROWS, 0:NJ * tw], m_scr[l])\
                          .then_inc(a.m_in, 16)
                    if prep:
                        stacks_in()
                steps(sp, step)
            sp.wait_ge(F[1].misc_free, F_USES)
            sp.dma_start(out, X[:, :, :]).then_inc(out_done, 16)
            sp.wait_ge(out_done, 16)

        @block.gpsimd
        def _(pool):
            pool.memset(zeros_m[:, :], 0.0).then_inc(zeros_ready, 1)
            pool.wait_ge(zeros_ready, 1)
            done = [0]

            def fill(dst, value):
                pool.memset(dst, value).then_inc(set_up, 1)
                done[0] += 1
                pool.wait_ge(set_up, done[0])

            fill(neg_half[:, :], -0.5)
            for k in range(2):
                fill(V[k][:, :, :, :], 0.0)
                fill(VX[k][:, :, :], 0.0)
                fill(KZ[k][SROWS:P, :, :, :], 0.0)
                fill(QS[k][SROWS:P, :], 0.0)
            fill(KC[SROWS:P, :, :], 0.0)
            for k in range(2):
                fill(V[k][:, :, :, D:D + 1], 1.0)
                fill(VX[k][0:64, :, D:D + 1], 1.0)
                fill(VX[k][64:P, :, 2 * D + 1:2 * D + 2], 1.0)
                fill(KZ[k][SROWS:SROWS + 3, :, 0, :], 1.0)
                fill(KZ[k][SROWS:SROWS + 6, :, 1, :], 1.0)
            fill(kc_sides[SROWS:SROWS + 3, :, 0, :], 1.0)
            fill(kc_sides[SROWS:SROWS + 6, :, 1, :], 1.0)
            for k in range(2):
                fill(KZ[k][SROWS:SROWS + 3, :, 1, :], 0.0)
            fill(kc_sides[SROWS:SROWS + 3, :, 1, :], 0.0)
            for c, e in ((cand0, E0), (cand1, E1)):
                fill(c[:, :, e:], -HUGE)
            for c, k in ((take0, K0), (take1, K1)):
                fill(c[:, :, k:], -HUGE)
            assert done[0] == SET_UP
            pool.wait_ge(x_in, 16)

            def rsqrt(f, i, n):
                wait_alone(pool, f.mv_ready, i + 1)
                pool.tensor_scalar(var_e[:, 0:n], mv[:, 0:n, 1], EPS, None, ALU.add).then_inc(f.rstd_chain, 1)
                pool.wait_ge(f.rstd_chain, i + 1)
                pool.tensor_tensor(rstd[:, 0:n], var_e[:, 0:n], neg_half[:, 0:n], ALU.pow).then_inc(f.rstd_ready, 1)

            for l in range(2):
                lay, a = LAYERS[l], A[l]
                tw = lay.tw
                per = 6 if lay.own else 3
                if l == 1:
                    pool.wait_ge(F[0].misc_free, F_USES)
                    for k in range(2):
                        pool.memset(QS[k][SROWS:P, 0:NJ * tw], 0.0).then_inc(stacks_zeroed, 1)
                        pool.wait_ge(stacks_zeroed, k + 1)

                def cut(src, parts, n, base, done):
                    pool.tensor_copy(parts[:, 0, 0:n], src[:, 0:n]).then_inc(a.cut_chain, 1)
                    pool.wait_ge(a.cut_chain, base + 1)
                    pool.tensor_tensor(rest[:, 0:n], src[:, 0:n], parts[:, 0, 0:n], ALU.subtract).then_inc(a.cut_chain, 1)
                    wait_alone(pool, a.cut_chain, base + 2)
                    pool.tensor_copy(parts[:, 1, 0:n], rest[:, 0:n]).then_inc(a.cut_chain, 1)
                    pool.wait_ge(a.cut_chain, base + 3)
                    pool.tensor_tensor(parts[:, 2, 0:n], rest[:, 0:n], parts[:, 1, 0:n], ALU.subtract).then_inc(done, 1)

                def step(s, par, prep, nat, trans, tail):
                    if prep:
                        rsqrt(a, s, 2)
                        wait_alone(pool, a.misc_free, lay.before(s, "Q") + 1)
                        wait_alone(pool, a.stack_written, s * (96 if lay.own else 48))
                        cut(qf, q_parts, tw, s * per, a.q_cut)
                        if lay.own:
                            wait_alone(pool, a.misc_free, lay.before(s, "KV") + 1)
                            cut(kf, k_parts, 2 * T, s * per + 3, a.k_cut)
                    if nat:
                        b = s - 1
                        wait_alone(pool, a.pv_done, (s - 2) * lay.units)
                        pool.wait_ge(vc_free, 8)
                        if prep:
                            wait_alone(pool, a.k_cut if lay.own else a.q_cut, s + 1)
                        elif lay.own:
                            wait_alone(pool, a.xb_ready, (s - 2) * 2)
                        src = VC[l][:, bass.ds(b, 1), :].rearrange("p b (j s d) -> p (b j) s d", s=2, d=D)
                        pool.tensor_copy(VX[1 - par][0:64, :, 0:D], src[0:64, :, 0, :]).then_inc(a.vx_ready, 1)
                        wait_alone(pool, a.vx_ready, b * 2 + 1)
                        pool.tensor_copy(VX[1 - par][64:P, :, D + 1:2 * D + 1], src[64:P, :, 1, :]).then_inc(a.vx_ready, 1)
                        wait_alone(pool, a.vx_ready, b * 2 + 2)
                    if trans and lay.own:
                        b = s - 2
                        if not isinstance(s, int) or b > 0:
                            pool.wait_ge(a.misc_free, lay.before(s, "O") + 1)
                        for i in range(2):
                            pool.tensor_tensor(xb[:, i, :], X[:, bass.ds(b * 2 + i, 1), :].rearrange("p a c -> p (a c)"),
                                               bp_row[:, :], ALU.add).then_inc(a.xb_ready, 1)

                steps(pool, step)
                f = F[l]
                pool.wait_ge(a.misc_free, lay.total)
                with pool.Fori(0, NCH) as c:
                    rsqrt(f, c, CT)

        @block.scalar
        def _(act):
            act.wait_ge(consts_in, CONSTS)
            act.wait_ge(bias_done, 4)
            for l in range(2):
                act.wait_ge(kc_full, l + 1)
                if l == 1:
                    act.wait_ge(kc_cut, 1)
                for s in range(2):
                    for h in range(2):
                        bias = bias_kz[:, 1, s:s + 1] if l == 0 else 0.0
                        o = kc_f[:, 1024 * h:1024 * h + 1024].rearrange("p (b s t) -> p b s t", s=2, t=TC)
                        act.activation(o[:, :, s, :], nat_ps[h][:, :].rearrange("p (b t) -> p b t", t=TC), ACT.Identity, bias=bias,
                                       scale=keep[:, s:s + 1]).then_inc(kc_flat, 1)
                for r in range(4):
                    act.wait_ge(vc_full, 4 * l + r + 1)
                    act.activation(VC[l][:, 4 * r:4 * r + 4, :].rearrange("p b c -> p (b c)"),
                                   [*tr_ps, *pv_ps[0:2]][r][:, :], ACT.Copy).then_inc(vc_free, 1)

            for l in range(2):
                lay, a = LAYERS[l], A[l]
                tw = lay.tw
                if l == 1:
                    act.wait_ge(F[0].misc_free, F_USES)
                act.wait_ge(set_up, SET_UP)

                def step(s, par, prep, nat, trans, tail):
                    for e in lay.order:
                        if not lay.live(e, prep, nat, trans, tail):
                            continue
                        if e in lay.uses and e not in ("O", "Y0", "Y1", "Y2"):
                            act.wait_ge(a.misc_full, lay.before(s, e) + 1)
                        if e[0] == "T":
                            j = int(e[1:])
                            n = (s - 2) * lay.units + j
                            if lay.own:
                                at_least(act, a.pv_done, n - 1)
                                for k in range(2):
                                    act.wait_ge(a.tr_full[k], n + 1)
                                    act.activation(PR[:, j % 2, k, :], tr_ps[k][:, :], ACT.Exp, scale=SCALE)\
                                       .then_inc(a.probs[k], 1)
                            else:
                                at_least(act, a.pv_done, n - 3)
                                k = j % 2
                                act.wait_ge(a.tr_full[k], (s - 2) * 2 + (j // 2 + 1))
                                act.activation(PR[:, j // 2, k, :], tr_ps[k][:, :], ACT.Exp, scale=SCALE)\
                                   .then_inc(a.probs[k], 1)
                        elif e == "XT":
                            act.activation(xt[par][:, :], misc[:, 0:T], ACT.Copy).then_inc(a.misc_free, 1)
                        elif e == "Q":
                            at_least(act, a.q_cut, s)
                            if lay.own:
                                act.activation(qf[:, 0:T], misc[:, 0:T], ACT.Identity, bias=bias_in[:, 0:1])
                                act.activation(qf[:, T:2 * T], misc[:, T:2 * T], ACT.Identity, bias=bias_in[:, 1:2])\
                                   .then_inc(a.misc_free, 1)
                            else:
                                act.activation(qf[:, 0:T], misc[:, 0:T], ACT.Copy).then_inc(a.misc_free, 1)
                        elif e == "KV":
                            last = None
                            if prep:
                                at_least(act, a.k_cut, s)
                                for i in range(2):
                                    last = act.activation(kf[:, T * i:T * i + T], misc[:, 0:T], ACT.Identity,
                                                          bias=bias_kz[:, 0, i:i + 1], scale=keep[:, i:i + 1])
                            if nat:
                                at_least(act, a.pv_done, (s - 2) * lay.units)
                                last = act.activation(V[1 - par][:, :, :, 0:D],
                                                      misc[:, T:2 * T].rearrange("p (k h d) -> p k h d", k=2, d=D), ACT.Copy)
                            last.then_inc(a.misc_free, 1)
                        elif e == "M":
                            at_least(act, a.m_written, (s - 1) * 16)
                            act.activation(mt[:, 0:tw], misc[0:48, :].bitcast(BF)[:, 0:tw], ACT.Copy).then_inc(a.misc_free, 1)
                        elif e in ("Y0", "Y1", "Y2"):
                            k = int(e[1])
                            act.wait_ge(a.pv_done, (s - 2) * lay.units + (4 if e == "Y0" else 0))
                            if e == "Y1":
                                act.wait_ge(a.misc_full, lay.before(s - 1, "Y0") + 1)
                            elif e == "Y2" and lay.own:
                                act.wait_ge(a.misc_full, lay.before(s, "Y1") + 1)
                            act.activation(yu[:, :], pv_ps[k][:, :], ACT.Copy).then_inc(a.yu_ready, 1)
                        elif e == "YT":
                            act.activation(yt[:, :], misc[:, 0:T], ACT.Identity, bias=bias_y[:, l:l + 1])\
                               .then_inc(a.misc_free, 1)

                steps(act, step)

                f = F[l]
                units = U0 if l == 0 else U1

                def prepare(what, par, c, used):
                    if what == "XT":
                        act.wait_ge(f.misc_full, used + 1)
                        act.activation(xt_f[:, par, :], misc[:, :], ACT.Copy).then_inc(f.misc_free, 1)
                    elif what == "R" and l == 0:
                        act.wait_ge(f.misc_full, used + 1)
                        act.activation(ex[:, :, :].rearrange("p t e -> p (t e)"), misc[:, 0:CT * E0], ACT.Exp,
                                       scale=-1.0).then_inc(f.misc_free, 1)
                    elif what == "R":
                        act.wait_ge(f.misc_free, used + 1)
                        act.activation(ex[:, :, 0:E1], sig[:, :, 0:E1], ACT.Exp).then_inc(f.ex_ready, 1)
                    elif what == "W":
                        act.wait_ge(f.misc_full, used + 1)
                        n = 3 * (E0 if l == 0 else E1)
                        act.activation(wt_f[par][0:n, :], misc[0:n, :].bitcast(BF)[:, 0:CH], ACT.Copy)\
                           .then_inc(f.misc_free, 1)

                taken = f.t_ready if l == 0 else f.h_ready

                def chunk(c, par, more):
                    for u in range(units):
                        n = c * units + u
                        slot = (par * units + u) % 2
                        at_least(act, taken, n - 1)
                        act.wait_ge(f.gate_full, n + 1)
                        act.activation(hid_s[:, slot, :], gate_ps[slot][:, :], ACT.Silu).then_inc(f.s_ready, 1)
                        for what, at, use in ROUTING[l]:
                            if at == u and more:
                                prepare(what, 1 - par, c + 1, c * 4 + use)
                    act.wait_ge(f.h_used, (c + 1) * units)
                    act.activation(yt_f, y_ps[:, :], ACT.Copy).then_inc(f.yt_ready, 1)

                act.wait_ge(a.misc_free, lay.total)
                act.wait_ge(f.wt_zeroed, 1)
                for i, what in enumerate(("XT", "R", "W")):
                    prepare(what, 0, 0, i)
                chunks(act, chunk)

        @block.vector
        def _(dve):
            dve.wait_ge(consts_in, CONSTS)
            dve.tensor_scalar(bias_kz[:, 0, :], keep[:, :], bias_in[:, 2:3], None, ALU.mult).then_inc(bias_done, 1)
            dve.tensor_scalar(bias_kz[:, 1, :], keep[:, :], bias_in[:, 3:4], None, ALU.mult).then_inc(bias_done, 1)
            dve.tensor_tensor(bias_y[:, 0:1], bias_in[:, 4:5], bias_in[:, 5:6], ALU.add).then_inc(bias_done, 1)
            dve.memset(bias_y[:, 1:2], 0.0).then_inc(bias_done, 1)
            for l in range(2):
                dve.wait_ge(kc_flat, 4 * l + 4)
                if l == 1:
                    dve.wait_ge(kc_written, 48)
                dve.tensor_copy(kc_parts[:, 0, :], kc_f).then_inc(kc_chain, 1)
                dve.wait_ge(kc_chain, 3 * l + 1)
                dve.tensor_tensor(kc_r, kc_f, kc_parts[:, 0, :], ALU.subtract).then_inc(kc_chain, 1)
                dve.wait_ge(kc_chain, 3 * l + 2)
                dve.tensor_copy(kc_parts[:, 1, :], kc_r).then_inc(kc_chain, 1)
                dve.wait_ge(kc_chain, 3 * l + 3)
                dve.tensor_tensor(kc_parts[:, 2, :], kc_r, kc_parts[:, 1, :], ALU.subtract).then_inc(kc_cut, 1)
            dve.wait_ge(x_in, 16)
            dve.wait_ge(set_up, SET_UP)

            def moments(f, i, first, n):
                at_least(dve, f.xn_ready, i)
                for k in range(n):
                    dve.bn_stats(stats[:, k, :], X[:, bass.ds(first + k, 1), :].rearrange("p a c -> p (a c)"))\
                       .then_inc(f.ln_chain, 1)
                wait_alone(dve, f.ln_chain, i * n + n)
                for k in range(n):
                    last = dve.bn_aggr(mv[:, k, :], stats[:, k, :])
                last.then_inc(f.mv_ready, 1)

            def normalize(f, i, first, n, dst, copied):
                dve.wait_ge(f.rstd_ready, i + 1)
                at_least(dve, f.misc_full, copied)
                for k in range(n):
                    last = dve.tensor_scalar(dst[:, k, :], X[:, bass.ds(first + k, 1), :].rearrange("p a c -> p (a c)"),
                                             mv[:, k, 0:1], rstd[:, k:k + 1], ALU.subtract, ALU.mult)
                last.then_inc(f.xn_ready, 1)

            for l in range(2):
                lay, a = LAYERS[l], A[l]
                kq = 2 * lay.kinds
                if l == 1:
                    dve.wait_ge(F[0].misc_free, F_USES)

                def step(s, par, prep, nat, trans, tail):
                    if prep:
                        moments(a, s, s * 2, 2)
                    for e in lay.order:
                        if e == "XT" and prep:
                            normalize(a, s, s * 2, 2, xn, lay.before(s - 1, "XT") + 1 if not isinstance(s, int) or s else 0)
                        if not lay.live(e, prep, nat, trans, tail):
                            continue
                        if e[0] == "N":
                            j = int(e[1:])
                            n = (s - 1) * lay.units + j
                            if j == 0:
                                at_least(dve, a.m_cut, s - 1)
                            if lay.own:
                                dve.wait_ge(a.nat_full[0], n + 1)
                                dve.tensor_reduce(nmax[:, 1, :, j], nat_ps[0][:, :].rearrange("p (s k) -> p s k", s=2),
                                                  AX.X, ALU.max, negate=True).then_inc(a.nat_free[0], 1)
                                dve.wait_ge(a.nat_full[1], n + 1)
                                dve.tensor_reduce(nmax[:, 0, :, j],
                                                  nat_ps[1][:, 0:T].rearrange("p (s k) -> p s k", s=2),
                                                  AX.X, ALU.max, negate=True)
                                dve.tensor_reduce(nmax[:, 2:4, :, j],
                                                  nat_ps[1][:, T:2 * T].rearrange("p (q s k) -> p q s k", q=2, s=2),
                                                  AX.X, ALU.max, negate=True).then_inc(a.nat_free[1], 1)
                            else:
                                dve.wait_ge(a.nat_full[j % 2], (s - 1) * 2 + (j // 2 + 1))
                                for i in range(2):
                                    last = dve.tensor_reduce(
                                        nmax[:, 0:2, :, 2 * j + i],
                                        nat_ps[j % 2][:, T * i:T * i + T].rearrange("p (q s k) -> p q s k", q=2, s=2),
                                        AX.X, ALU.max, negate=True)
                                last.then_inc(a.nat_free[j % 2], 1)
                            if j == lay.units - 1:
                                k = lay.units // 2 if not lay.own else lay.units
                                for q in range(2):
                                    dve.wait_ge(a.nat_free[q], s * k)
                                if not isinstance(s, int) or s > 1:
                                    dve.wait_ge(a.misc_full, lay.before(s - 1, "M") + 1)
                                c3 = (s - 1) * 3
                                src, rest = nmax[:, 0:kq, :, :], nmax_r[:, 0:kq, :, :]
                                dve.tensor_copy(nmax_p[:, 0:kq, :, 0, :], src).then_inc(a.m_chain, 1)
                                dve.wait_ge(a.m_chain, c3 + 1)
                                dve.tensor_tensor(rest, src, nmax_p[:, 0:kq, :, 0, :], ALU.subtract).then_inc(a.m_chain, 1)
                                dve.wait_ge(a.m_chain, c3 + 2)
                                dve.tensor_copy(nmax_p[:, 0:kq, :, 1, :], rest).then_inc(a.m_chain, 1)
                                dve.wait_ge(a.m_chain, c3 + 3)
                                dve.tensor_tensor(nmax_p[:, 0:kq, :, 2, :], rest, nmax_p[:, 0:kq, :, 1, :], ALU.subtract)\
                                   .then_inc(a.m_cut, 1)
                        elif e in ("Y0", "Y1"):
                            k = int(e[1])
                            c = (s - 2 - k) * 4 + k
                            dve.wait_ge(a.misc_full, lay.before(s, e) + 1)
                            o = misc[:, :].rearrange("p (q h n) -> p q h n", q=2, n=32)
                            inv = den[:, 0:16].rearrange("p (q h) -> p q h", q=2).unsqueeze(3)
                            dve.reciprocal(inv, o[:, :, :, D:D + 1]).then_inc(a.y_chain, 1)
                            dve.wait_ge(a.y_chain, c + 1)
                            dst = y_own[:, :, 64 * k:64 * k + 64].rearrange("p q (h d) -> p q h d", d=D)
                            dve.tensor_tensor(dst, o[:, :, :, 0:D], inv.broadcast_to([P, 2, 8, D]), ALU.mult)\
                               .then_inc(a.misc_free, 1)
                        elif e == "Y2":
                            per = 4 if lay.own else 2
                            c = (s - 3) * per + (2 if lay.own else 0)
                            dve.wait_ge(a.misc_full, lay.before(s, e) + 1)
                            dst = y_ctx if lay.own else y_all
                            o = misc[:, :].rearrange("p (q h n) -> p q h n", q=2, n=32)
                            for i in range(2):
                                inv = den[:, 16 * i:16 * i + 16].rearrange("p (q h) -> p q h", q=2).unsqueeze(3)
                                v = i * (D + 1)
                                dve.reciprocal(inv, o[:, :, :, v + D:v + D + 1]).then_inc(a.y_chain, 1)
                            dve.wait_ge(a.y_chain, c + 2)
                            for i in range(2):
                                inv = den[:, 16 * i:16 * i + 16].rearrange("p (q h) -> p q h", q=2).unsqueeze(3)
                                v = i * (D + 1)
                                dd = dst[:, :, :].rearrange("p q (h s d) -> p q h s d", s=2, d=D)[:, :, :, i, :]
                                last = dve.tensor_tensor(dd, o[:, :, :, v:v + D], inv.broadcast_to([P, 2, 8, D]), ALU.mult)
                            last.then_inc(a.misc_free, 1)
                            if lay.own:
                                dve.wait_ge(a.misc_free, lay.before(s, e) + 1)
                                dve.tensor_tensor(y_all[:, :, :], y_own[:, :, :], y_ctx[:, :, :], ALU.add)\
                                   .then_inc(a.y_ready, 1)
                        elif e == "O":
                            dve.wait_ge(a.misc_full, lay.before(s, e) + 1)
                            x2 = X[:, bass.ds((s - 3) * 2, 2), :]
                            if lay.own:
                                dve.wait_ge(a.xb_ready, (s - 2) * 2)
                            dve.tensor_tensor(x2, misc[:, 0:T].rearrange("p (i c) -> p i c", i=2),
                                              xb[:, :, :] if lay.own else x2, ALU.add).then_inc(a.misc_free, 1)

                steps(dve, step)
                f = F[l]
                units = U0 if l == 0 else U1
                dve.wait_ge(a.misc_free, lay.total)
                for k in range(2):
                    last = dve.memset(wt_f[k], 0.0)
                last.then_inc(f.wt_zeroed, 1)
                taken = f.t_ready if l == 0 else f.h_ready

                total = ROUTE_LINKS[l]
                links = [0]

                wait = lambda eng, sem, value: eng.wait_ge(sem, value)

                def link(c, ins, apart=False):
                    links[0] += 1
                    ins.then_inc(f.r_chain, 1)
                    (wait_alone if apart else wait)(dve, f.r_chain, c * total + links[0])

                def route(c, used, part):
                    ne, nk = (E0, K0) if l == 0 else (E1, K1)
                    cand, mark, take = (cand0, mark0, take0) if l == 0 else (cand1, mark1, take1)
                    s_, w_, r_ = sig[:, :, 0:ne], wgt[:, :, 0:ne], wrest[:, :, 0:ne]
                    per = E0 // G0
                    tg = top_g[:, :, :].rearrange("p (t g) n -> p t g n", t=CT)
                    if part == 0:
                        links[0] = 0
                        if not isinstance(c, int) or c:
                            dve.wait_ge(f.w_cut, c)
                            dve.wait_ge(f.misc_full, used - 1)
                    if l == 0 and part == 0:
                        dve.wait_ge(f.misc_free, used + 1)
                        link(c, dve.tensor_scalar(ex[:, :, :], ex[:, :, :], 1.0, None, ALU.add))
                        link(c, dve.reciprocal(s_, ex[:, :, :]))
                        bias = router_bias[:, :].unsqueeze(1).broadcast_to([P, CT, E0])
                        link(c, dve.tensor_tensor(biased[:, :, :], s_, bias, ALU.add), apart=True)
                    elif l == 0 and part in (1, 2):
                        half = CT * G0 // 2
                        for g in range((part - 1) * half, part * half):
                            last = dve.max(top_g[:, g, :], biased[:, g // G0, per * (g % G0):per * (g % G0) + per])
                        if part == 2:
                            link(c, last)
                            link(c, dve.tensor_tensor(gs[:, :, :].unsqueeze(3), tg[:, :, :, 0:1], tg[:, :, :, 1:2], ALU.add))
                    elif l == 0 and part == 3:
                        for k in range(CT):
                            other = gs[:, k, :].unsqueeze(1).broadcast_to([P, G0, G0])
                            this = gs[:, k, :].unsqueeze(2).broadcast_to([P, G0, G0])
                            dve.tensor_tensor(cmp_a[:, k, :, :], other, this, ALU.is_gt)
                            last = dve.tensor_tensor(cmp_b[:, k, :, :], other, this, ALU.is_equal)
                        link(c, last)
                        low = lower[:, :, :].rearrange("p a b -> p (a b)").unsqueeze(1).broadcast_to([P, CT, G0 * G0])
                        ca, cb = (x[:, :, :, :].rearrange("p t a b -> p t (a b)") for x in (cmp_a, cmp_b))
                        link(c, dve.tensor_tensor(cb, cb, low, ALU.mult))
                    elif l == 0 and part == 4:
                        ca, cb = (x[:, :, :, :].rearrange("p t a b -> p t (a b)") for x in (cmp_a, cmp_b))
                        link(c, dve.tensor_tensor(ca, ca, cb, ALU.add))
                        link(c, dve.tensor_reduce(rank[:, :, :], cmp_a[:, :, :, :], AX.X, ALU.add))
                        link(c, dve.tensor_scalar(gmask[:, :, :], rank[:, :, :], 1.5, None, ALU.is_lt))
                        for k in range(CT):
                            last = dve.tensor_tensor(cand[:, k, 0:ne].rearrange("p (g e) -> p g e", g=G0),
                                                     biased[:, k, :].rearrange("p (g e) -> p g e", g=G0),
                                                     gmask[:, k, :].unsqueeze(2).broadcast_to([P, G0, per]), ALU.mult)
                        link(c, last, apart=True)
                    elif l == 1 and part == 0:
                        dve.wait_ge(f.misc_full, used + 1)
                        lg = misc[:, 0:CT * ne].rearrange("p (t e) -> p t e", e=ne)
                        spread = lambda x: x[:, :].unsqueeze(2).broadcast_to([P, CT, ne])
                        link(c, dve.tensor_reduce(wsum[:, :], lg, AX.X, ALU.max))
                        dve.tensor_tensor(s_, lg, spread(wsum), ALU.subtract).then_inc(f.misc_free, 1)
                        dve.wait_ge(f.ex_ready, c + 1)
                        link(c, dve.tensor_reduce(wsum[:, :], ex[:, :, 0:ne], AX.X, ALU.add))
                        link(c, dve.reciprocal(winv[:, :], wsum[:, :]))
                        dve.tensor_tensor(s_, ex[:, :, 0:ne], spread(winv), ALU.mult)
                        link(c, dve.tensor_tensor(cand[:, :, 0:ne], ex[:, :, 0:ne], spread(winv), ALU.mult), apart=True)
                    elif part == 5:
                        for k in range(CT):
                            last = dve.max(top[:, k, :], cand[:, k, 0:ne])
                        link(c, last)
                        link(c, dve.tensor_copy(take[:, :, 0:nk], top[:, :, 0:nk]), apart=True)
                        for k in range(CT):
                            last = dve.match_replace(out=mark[:, k, :], in_to_replace=take[:, k, :],
                                                     in_values=cand[:, k, :], imm_value=HUGE)
                        link(c, last)
                        link(c, dve.tensor_scalar(wsel[:, :, 0:ne], mark[:, :, 0:ne], HUGE / 2, None, ALU.is_gt))
                    elif part == 6:
                        link(c, dve.tensor_tensor(w_, s_, wsel[:, :, 0:ne], ALU.mult))
                        link(c, dve.tensor_reduce(wsum[:, :], w_, AX.X, ALU.add))
                        if l == 0:
                            link(c, dve.tensor_scalar(wsum[:, :], wsum[:, :], 1e-20, None, ALU.add))
                        link(c, dve.reciprocal(winv[:, :], wsum[:, :]))
                        link(c, dve.scalar_tensor_tensor(out=w_, in0=w_, scalar=ROUTE_SCALE if l == 0 else 1.0,
                                                         in1=winv[:, :].unsqueeze(2).broadcast_to([P, CT, ne]),
                                                         op0=ALU.mult, op1=ALU.mult))
                    elif part == 7:
                        wp = w_parts[:, :, 0:3 * ne].rearrange("p t (r e) -> p t r e", r=3)
                        link(c, dve.tensor_copy(wp[:, :, 0, :], w_))
                        link(c, dve.tensor_tensor(r_, w_, wp[:, :, 0, :], ALU.subtract))
                        link(c, dve.tensor_copy(wp[:, :, 1, :], r_))
                        dve.tensor_tensor(wp[:, :, 2, :], r_, wp[:, :, 1, :], ALU.subtract).then_inc(f.w_cut, 1)
                        assert links[0] == total, links[0]

                def weighted_x(c, par, e):
                    dve.wait_ge(f.wb_full, c * E1 + (e + 1))
                    at_least(dve, f.up_full, c * units + 4 * (e - 1))
                    dve.tensor_tensor(xw[:, e % 2, :], xt_f[:, par, :], wb_ps[e % 2][:, :], ALU.mult)\
                       .then_inc(f.xw_ready, 1)

                def residual(c, used):
                    dve.wait_ge(f.misc_full, used + 1)
                    x4 = X[:, bass.ds(c * CT, CT), :]
                    dve.tensor_tensor(x4, misc[:, :].rearrange("p (t c) -> p t c", t=CT), x4, ALU.add)\
                       .then_inc(f.misc_free, 1)

                def chunk(c, par, more):
                    if l == 1:
                        weighted_x(c, par, 0)
                    for u in range(units):
                        n = c * units + u
                        slot = (par * units + u) % 2
                        if u == LN_AT and more:
                            moments(f, c + 1, (c + 1) * CT, CT)
                        if u == LN_AT + 1 and more:
                            normalize(f, c + 1, (c + 1) * CT, CT, xn_f, c * 4 + (0 if not isinstance(c, int) or c else 1))
                        dve.wait_ge(f.s_ready, n + 1)
                        dve.wait_ge(f.up_full, n + 1)
                        at_least(dve, f.h_used, n - 1)
                        if l == 0:
                            at_least(dve, f.h_ready, n - 1)
                            dve.tensor_tensor(hid_t[:, slot, :], hid_s[:, slot, :], up_ps[slot][:, :], ALU.mult)\
                               .then_inc(f.t_ready, 1)
                            dve.wait_ge(f.t_ready, n + 1)
                            if u < units - 1:
                                dve.wait_ge(f.wb_full, c * (units - 1) + (u + 1))
                                dve.tensor_tensor(hid_h[:, slot, :], hid_t[:, slot, :], wb_ps[u % 2][:, :], ALU.mult)\
                                   .then_inc(f.h_ready, 1)
                            else:
                                dve.tensor_copy(hid_h[:, slot, :], hid_t[:, slot, :]).then_inc(f.h_ready, 1)
                        else:
                            dve.tensor_tensor(hid_h[:, slot, :], hid_s[:, slot, :], up_ps[slot][:, :], ALU.mult)\
                               .then_inc(f.h_ready, 1)
                            if u % 4 == 1 and u // 4 + 1 < E1:
                                weighted_x(c, par, u // 4 + 1)
                        if u == Y_AT and (not isinstance(c, int) or c):
                            residual(c - 1, c * 4 + 2)
                        part = u - ROUTING[l][1][1]
                        if 0 <= part < ROUTE_PARTS and more:
                            route(c + 1, c * 4 + 4, part)

                moments(f, 0, 0, CT)
                normalize(f, 0, 0, CT, xn_f, 0)
                for part in range(ROUTE_PARTS):
                    route(0, 1, part)
                chunks(dve, chunk)
                residual(NCH - 1, F_USES - 1)

        @block.tensor
        def _(pe):
            pe.wait_ge(consts_in, CONSTS)
            pe.wait_ge(ctx_in, 16)
            for l in range(2):
                if l == 1:
                    pe.wait_ge(kc_flat, 4)
                for h in range(2):
                    last = pe.matmul(nat_ps[h][:, :], w_ctx[:, l, 0, :], ctx_t[0:CC, 512 * h:512 * h + 512],
                                     start=True, stop=True)
                last.then_inc(kc_full, 1)
                for r in range(4):
                    at_least(pe, vc_free, 4 * (l - 1) + r + 1)
                    for k in range(4):
                        src = ctx_t[0:CC, TC * (4 * r + k):TC * (4 * r + k) + TC]
                        for half in range(2):
                            last = pe.matmul([*tr_ps, *pv_ps[0:2]][r][64 * half:64 * half + 64, P * k:P * k + P], src,
                                             w_ctx[:, l, 1, :], start=True, stop=True)
                    last.then_inc(vc_full, 1)

            for l in range(2):
                lay, a = LAYERS[l], A[l]
                tw, qc = lay.tw, lay.qc
                pe.wait_ge(kc_in, 16 * (l + 1))
                pe.wait_ge(set_up, SET_UP)
                pe.wait_ge(vc_free, 8)
                if l == 1:
                    pe.wait_ge(F[0].misc_free, F_USES)
                wa = w_att[l]

                def step(s, par, prep, nat, trans, tail):
                    q_nat, q_tr = stack_in_cols(QS[1 - par], tw), stack_in_cols(QS[par], tw)
                    kz_nat, kz_tr = KZ[1 - par], KZ[par]
                    for e in lay.order:
                        if not lay.live(e, prep, nat, trans, tail):
                            continue
                        if e in lay.uses:
                            at_least(pe, a.misc_free, lay.before(s, e))
                        if e[0] == "N":
                            b, u = s - 1, int(e[1:])
                            n = b * lay.units + u
                            if u == 0:
                                pe.wait_ge(a.stack_in, s * (32 if lay.own else 16))
                            if lay.own:
                                at_least(pe, a.nat_free[0], n)
                                o = nat_ps[0][:, :].rearrange("p (s k) -> p s k", s=2)
                                pe.matmul(nat_ps[0][:, :], q_nat[:, u, P:T], kz_nat[:, u, :, :], start=True, stop=False,
                                          skip_group_check=True)
                                pe.matmul(o[:, :, P:T], identb[:, :], mask_nat[:, :, :], start=False, stop=True,
                                          skip_group_check=True).then_inc(a.nat_full[0], 1)
                                at_least(pe, a.nat_free[1], n)
                                pe.matmul(nat_ps[1][:, 0:T], q_nat[:, u, 0:P], kz_nat[:, u, :, 0:P], start=True,
                                          stop=False, skip_group_check=True)
                                pe.matmul(nat_ps[1][:, 0:T], identb[:, :], mask_nat[:, :, :], start=False, stop=True,
                                          skip_group_check=True)
                                for q in range(2):
                                    last = pe.matmul(nat_ps[1][:, T + P * q:T + P * q + P],
                                                     q_nat[:, u, qc + P * q:qc + P * q + P],
                                                     KC[:, u, bass.ds(b * 2 * TC, 2 * TC)], start=False, stop=True,
                                                     skip_group_check=True)
                                last.then_inc(a.nat_full[1], 1)
                            else:
                                k = u % 2
                                at_least(pe, a.nat_free[k], b * 2 + u // 2)
                                for i in range(2):
                                    for q in range(2):
                                        at = T * i + P * q
                                        last = pe.matmul(nat_ps[k][:, at:at + P], q_nat[:, 2 * u + i, P * q:P * q + P],
                                                         KC[:, 2 * u + i, bass.ds(b * 2 * TC, 2 * TC)], start=True, stop=True)
                                last.then_inc(a.nat_full[k], 1)
                        elif e[0] == "T":
                            b, u = s - 2, int(e[1:])
                            n = b * lay.units + u
                            if u == 0:
                                pe.wait_ge(a.m_in, (s - 1) * 16)
                            if lay.own:
                                at_least(pe, a.probs[0], n)
                                for i in range(2):
                                    pe.matmul(tr_ps[0][:, T * i:T * i + T], kz_tr[:, u, i, 0:P], q_tr[:, u, 0:T],
                                              start=(i == 0), stop=False, skip_group_check=True)
                                o = tr_ps[0][:, :].rearrange("p (s k) -> p s k", s=2)
                                pe.matmul(o[:, :, 0:P], identb[:, :], mask_tr[:, :, :], start=False, stop=True,
                                          skip_group_check=True).then_inc(a.tr_full[0], 1)
                                at_least(pe, a.probs[1], n)
                                for i in range(2):
                                    pe.matmul(tr_ps[1][:, P * i:P * i + P], kz_tr[:, u, i, P:T], q_tr[:, u, P:T],
                                              start=(i == 0), stop=False, skip_group_check=True)
                                pe.matmul(tr_ps[1][:, 0:T], identb[:, :], mask_tr[:, :, :], start=False, stop=True,
                                          skip_group_check=True)
                                pe.matmul(tr_ps[1][:, T:2 * T], KC[:, u, bass.ds(b * 2 * TC, 2 * TC)], q_tr[:, u, qc:qc + T],
                                          start=False, stop=True, skip_group_check=True).then_inc(a.tr_full[1], 1)
                            else:
                                k = u % 2
                                at_least(pe, a.probs[k], b * 2 + u // 2)
                                for i in range(2):
                                    last = pe.matmul(tr_ps[k][:, T * i:T * i + T], KC[:, 2 * u + i, bass.ds(b * 2 * TC, 2 * TC)],
                                                     q_tr[:, 2 * u + i, 0:T], start=True, stop=True)
                                last.then_inc(a.tr_full[k], 1)
                        elif e[0] == "P":
                            b, u = s - 2, int(e[1:])
                            n = b * lay.units + u
                            if u == 0:
                                pe.wait_ge(a.vx_ready, (s - 1) * 2)
                                at_least(pe, a.yu_ready, b * (3 if lay.own else 1))
                            if lay.own:
                                pe.wait_ge(a.probs[0], n + 1)
                                pe.wait_ge(a.probs[1], n + 1)
                                cols = T * ((u // 2) % 2)
                                for kb in range(2):
                                    for i in range(2):
                                        row = 32 * (2 * (u % 2) + i)
                                        pe.matmul(pv_ps[u // 4][row:row + 32, cols + P * kb:cols + T],
                                                  V[par][:, kb, 2 * u + i, :],
                                                  PR[:, u % 2, kb, (T if kb == 0 else P) * i:(T if kb == 0 else P) * (i + 1)],
                                                  start=(kb == 0), stop=(kb == 1), skip_group_check=True)
                                pairs = [(u, PR[:, u % 2, 1, T:2 * T])]
                            else:
                                pe.wait_ge(a.probs[u % 2], b * 2 + (u // 2 + 1))
                                pairs = [(2 * u + i, PR[:, u // 2, u % 2, T * i:T * i + T]) for i in range(2)]
                            for j, probs in pairs:
                                row, cols = 32 * (j % 4), T * (j // 4)
                                last = pe.matmul(pv_ps[2][row:row + 32, cols:cols + T], VX[par][:, j, :], probs,
                                                 start=True, stop=True)
                            last.then_inc(a.pv_done, 1)
                        elif e == "XT":
                            pe.wait_ge(a.xn_ready, s + 1)
                            for i in range(2):
                                last = pe.transpose(misc[:, P * i:P * i + P], xn[:, i, :], identf[:, :])
                            last.then_inc(a.misc_full, 1)
                        elif e == "Q":
                            for i in range(lay.kinds):
                                last = pe.matmul(misc[:, T * i:T * i + T], wa[:, i, :], xt[par][:, :], start=True, stop=True)
                            last.then_inc(a.misc_full, 1)
                        elif e == "KV":
                            if prep:
                                last = pe.matmul(misc[:, 0:T], wa[:, 2, :], xt[par][:, :], start=True, stop=True)
                            if nat:
                                for i in range(2):
                                    last = pe.matmul(misc[:, T + P * i:T + P * i + P], xt[1 - par][:, P * i:P * i + P],
                                                     wa[:, 3, :], start=True, stop=True)
                            last.then_inc(a.misc_full, 1)
                        elif e == "M":
                            wait_alone(pe, a.m_cut, s)
                            for i in range(2 * lay.kinds):
                                last = pe.transpose(misc[0:48, :].bitcast(BF)[:, P * i:P * i + P],
                                                    nmax_p[:, i, :, :, :].rearrange("p s r j -> p (s r j)"), identb[:, :])
                            last.then_inc(a.misc_full, 1)
                        elif e in ("Y0", "Y1", "Y2"):
                            k = int(e[1])
                            b = s - (2 if k == 0 else 3)
                            pe.wait_ge(a.yu_ready, b * 3 + (k + 1) if lay.own else b + 1)
                            for q in range(2):
                                for g in range(2):
                                    at = P * (2 * q + g)
                                    last = pe.transpose(misc[:, at:at + P], yu[:, T * g + P * q:T * g + P * q + P],
                                                        identf[:, :])
                            last.then_inc(a.misc_full, 1)
                        elif e == "YT":
                            if lay.own:
                                pe.wait_ge(a.y_ready, s - 2)
                            for i in range(2):
                                last = pe.transpose(misc[:, P * i:P * i + P], y_all[:, i, :], identf[:, :])
                            last.then_inc(a.misc_full, 1)
                        elif e == "O":
                            for i in range(2):
                                last = pe.matmul(misc[:, P * i:P * i + P], yt[:, P * i:P * i + P], wa[:, 4 if lay.own else 1, :],
                                                 start=True, stop=True)
                            last.then_inc(a.misc_full, 1)

                steps(pe, step)
                f = F[l]
                units = U0 if l == 0 else U1
                taken = f.t_ready if l == 0 else f.h_ready
                if l == 0:
                    pe.wait_ge(gu0_in, 48)
                else:
                    pe.wait_ge(w1_in, 32)

                def prepare(what, c, par, used):
                    at_least(pe, f.misc_free, used)
                    if what == "XT":
                        pe.wait_ge(f.xn_ready, c + 1)
                        for i in range(CT):
                            last = pe.transpose(misc[:, P * i:P * i + P], xn_f[:, i, :], identf[:, :])
                    elif what == "R":
                        w, ne = (w_router0, E0) if l == 0 else (w_router1, E1)
                        for i in range(CT):
                            last = pe.matmul(misc[:, ne * i:ne * i + ne], xt_f[:, par, P * i:P * i + P], w[:, :],
                                             start=True, stop=True)
                    else:
                        pe.wait_ge(f.w_cut, c + 1)
                        n = 3 * (E0 if l == 0 else E1)
                        for i in range(CT):
                            last = pe.transpose(misc[0:n, :].bitcast(BF)[:, P * i:P * i + P], w_parts[:, i, 0:n], identb[:, :])
                    last.then_inc(f.misc_full, 1)

                def output(c, used):
                    at_least(pe, f.misc_free, used)
                    pe.wait_ge(f.yt_ready, c + 1)
                    for i in range(CT):
                        last = pe.transpose(misc[:, P * i:P * i + P], yt_f[:, P * i:P * i + P], identf[:, :])
                    last.then_inc(f.misc_full, 1)

                def spread(c, par, e):
                    if l == 0:
                        at_least(pe, f.h_ready, c * units + e - 1)
                    else:
                        at_least(pe, f.xw_ready, c * E1 + (e - 1))
                    pe.matmul(wb_ps[e % 2][:, :], (sel0 if l == 0 else sel1)[:, e, :], wt_f[par], start=True, stop=True)\
                      .then_inc(f.wb_full, 1)

                def chunk(c, par, more):
                    pe.wait_ge(f.misc_free, 3 if isinstance(c, int) and c == 0 else c * 4 + 2)
                    if l == 1:
                        spread(c, par, 0)
                    for u in range(units + 1):
                        n = c * units + u
                        slot = (par * units + u) % 2
                        if u < units:
                            if l == 0:
                                w_gate, w_up, x_up = w_gate0[:, u, :], w_up0[:, u, :], xt_f[:, par, :]
                            else:
                                w_gate, w_up = w_gu1[:, u // 4, 0, u % 4, :], w_gu1[:, u // 4, 1, u % 4, :]
                                x_up = xw[:, (u // 4) % 2, :]
                            at_least(pe, f.s_ready, n - 1)
                            pe.matmul(gate_ps[slot][:, :], w_gate, xt_f[:, par, :], start=True, stop=True)\
                              .then_inc(f.gate_full, 1)
                            at_least(pe, taken, n - 1)
                            if l == 1 and u % 4 == 0:
                                pe.wait_ge(f.xw_ready, c * E1 + (u // 4 + 1))
                            pe.matmul(up_ps[slot][:, :], w_up, x_up, start=True, stop=True).then_inc(f.up_full, 1)
                            if l == 0 and u < units - 1:
                                spread(c, par, u)
                            if l == 1 and u % 4 == 1 and u // 4 + 1 < E1:
                                spread(c, par, u // 4 + 1)
                        if u:
                            if u == 1:
                                at_least(pe, f.yt_ready, c)
                            pe.wait_ge(f.h_ready, n)
                            w_down = w_down0[:, u - 1, :] if l == 0 else w_dn1[:, u - 1, :]
                            pe.matmul(y_ps[:, :], w_down, hid_h[:, 1 - slot, :], start=(u == 1), stop=(u == units))\
                              .then_inc(f.h_used, 1)
                        if u == Y_AT and (not isinstance(c, int) or c):
                            output(c - 1, c * 4 + 2)
                        for what, at, use in ROUTING[l]:
                            if at == u and more:
                                prepare(what, c + 1, 1 - par, c * 4 + use)

                for i, what in enumerate(("XT", "R", "W")):
                    prepare(what, 0, 0, i)
                chunks(pe, chunk)
                output(NCH - 1, F_USES - 1)


_INS = ("c_identf", "c_identb", "c_keep", "c_mask_nat", "c_mask_tr", "c_lower", "c_sel0", "c_sel1", "biases", "w_att0",
        "w_att1", "w_ctx", "w_router0", "w_router1", "bp", "router_bias", "ctx", "x", "w_gate0", "w_up0", "w_down0",
        "w_gu1", "w_dn1")


def kernel(**inputs):
    import ml_dtypes as _ml
    import numpy as _np
    import concourse.bacc as _bacc
    from concourse import mybir as _mybir
    from concourse.bass_utils import run_bass_kernel_spmd as _run

    g = {k: _np.asarray(v) for k, v in inputs.items()}
    f32, bf16 = _np.float32, _ml.bfloat16
    perm = _np.array([(2 * j + s) * D + d for s in range(2) for d in range(D) for j in range(NJ)])
    heads = lambda w: w[:, perm]
    a = {}
    a["c_identf"] = _np.eye(P, dtype=f32)
    a["c_identb"] = _np.eye(P, dtype=f32).astype(bf16)
    a["c_keep"] = _np.stack([_np.arange(P) < 64, _np.arange(P) >= 64], 1).astype(f32)
    later = _np.triu(_np.full((P, P), MASKED, f32), 1)
    a["c_mask_nat"] = _np.stack([later, later], 1).astype(bf16)
    a["c_mask_tr"] = _np.stack([later.T, later.T], 1).astype(bf16)
    a["c_lower"] = _np.broadcast_to(_np.tril(_np.ones((G0, G0), f32), -1), (P, G0, G0))
    for name, ne, per in (("c_sel0", E0, P // I0), ("c_sel1", E1, 1)):
        sel = _np.zeros((P, ne // per, P), f32)
        for r in range(3):
            for e in range(ne):
                w = P // per
                sel[r * ne + e, e // per, (e % per) * w:(e % per) * w + w] = 1
        a[name] = sel.astype(bf16)
    a["biases"] = _np.stack([g["L0_xattn_bq"][perm], g["L0_xattn_bcq"][perm], g["L0_xattn_bk"][perm],
                             g["L0_xattn_bck"][perm], g["L0_xattn_bv"], g["L0_xattn_bcv"]], 1)
    a["w_att0"] = _np.stack([heads(g["L0_xattn_Wq"]), heads(g["L0_xattn_Wcq"]), heads(g["L0_xattn_Wk"]),
                             g["L0_xattn_Wv"], g["L0_xattn_Wp"]], 1)
    a["w_att1"] = _np.stack([heads(g["L1_xattn_Wq"].T), g["L1_xattn_Wo"].T], 1)
    kv1 = g["L1_xattn_Wkv"].T
    a["w_ctx"] = _np.stack([_np.stack([heads(g["L0_xattn_Wck"]), g["L0_xattn_Wcv"]], 1),
                            _np.stack([heads(kv1[:, 0:C]), kv1[:, C:2 * C]], 1)], 1)
    a["w_router0"], a["w_router1"] = g["L0_ffn_router_weight"].T, g["L1_ffn_gate_w"].T
    a["bp"], a["router_bias"] = g["L0_xattn_bp"], g["L0_ffn_router_bias"]
    a["ctx"] = g["ctx_512"].reshape(NCTX, CC).T
    a["x"] = g["x"].reshape(NT, P, C).transpose(1, 0, 2)
    units = lambda w, s: _np.concatenate([w.reshape(E0 * I0, C), s]).T.reshape(C, U0, P)
    a["w_gate0"] = units(g["L0_ffn_gate_w"], g["L0_ffn_shared_gate_w"])
    a["w_up0"] = units(g["L0_ffn_up_w"], g["L0_ffn_shared_up_w"])
    down = _np.concatenate([g["L0_ffn_down_w"].transpose(0, 2, 1).reshape(E0 * I0, C), g["L0_ffn_shared_down_w"].T])
    a["w_down0"] = down.reshape(U0, P, C).transpose(1, 0, 2)
    a["w_gu1"] = g["L1_ffn_gate_up_proj"].reshape(E1, 2, 4, P, C).transpose(4, 0, 1, 2, 3)
    a["w_dn1"] = g["L1_ffn_down_proj"].transpose(0, 2, 1).reshape(U1, P, C).transpose(1, 0, 2)

    nc = _bacc.Bacc("TRN2", target_bir_lowering=False, num_devices=1)
    arrays, aps = {}, {}
    for name in _INS:
        v = _np.ascontiguousarray(a[name])
        arrays[f"in_{name}"] = v
        aps[name] = nc.dram_tensor(f"in_{name}", v.shape, _mybir.dt.from_np(v.dtype), kind="ExternalInput").ap()
    out = nc.dram_tensor("out_0", (P, NT, C), _mybir.dt.float32, kind="ExternalOutput").ap()
    bass_two_layers(nc, aps, out)
    r = _run(nc, [arrays], core_ids=[0])
    got = r.results[0]["out_0"]
    return got.transpose(1, 0, 2).reshape(B, T, C)
```

```python
from contextlib import ExitStack

import numpy as np

import concourse.bass as bass
from concourse import mybir

F32 = mybir.dt.float32
BF = mybir.dt.bfloat16
I32, U32 = mybir.dt.int32, mybir.dt.uint32
ALU = mybir.AluOpType
ACT = mybir.ActivationFunctionType
AX = mybir.AxisListType

P = 128
B, T, C = 16, 256, 128
TC, CC = 64, 64
H, D = 16, 8
NJ = H // 2
NT = B * T // P
NCTX = B * TC
SCALE = float(np.float32(1.0 / np.sqrt(D)))
EPS = 1e-5
SLOTS = 6
SROWS = SLOTS * 16
MROWS = 6
MASKED = -1e38
HUGE = 3e38
E0, I0, K0, G0 = 32, 64, 4, 4
ROUTE_SCALE = 2.5
E1, I1, K1 = 8, 512, 2
CH = 512
NCH = B * T // CH
CT = CH // P
U0 = E0 * I0 // P + 1
ST = NT * K1 + E1 - 1
ST += -ST % 4
NBUF = 4
GBUF = 8


class Layer:

    def __init__(self, own, order):
        self.own = own
        self.order = order
        self.kinds = 2 if own else 1
        self.tw = T * self.kinds
        self.qc = T if own else 0
        self.units = NJ if own else NJ // 2
        self.uses = [e for e in order if e in ("XT", "Q", "KV", "M", "Y0", "Y1", "Y2", "YT", "O")]

        self.total = self.before(B + 2, "O") + 1

    def live(self, e, prep, nat, trans, tail):
        if e in ("XT", "Q"):
            return prep
        if e == "KV":
            return prep or nat
        if e[0] in "NM":
            return nat
        if e in ("Y1", "Y2", "YT", "O"):
            return tail
        return trans

    def before(self, s, e):
        count = 0
        if isinstance(s, int):
            parts = lambda t: (t < B, 0 <= t - 1 < B, 0 <= t - 2 < B, 0 <= t - 3 < B)
            for t in range(s):
                count += sum(self.live(u, *parts(t)) for u in self.uses)
            for u in self.uses:
                if u == e:
                    return count
                count += self.live(u, *parts(s))
        three = self.before(3, self.uses[0])
        return (s - 3) * len(self.uses) + (three + self.uses.index(e))


F_USES = 4 * NCH
CONSTS = 16 * 18
SET_UP = 13
ROUTING = [("XT", 2, 3), ("R", 4, 4), ("W", 13, 5)]
LN_AT, Y_AT = 0, 1
ROUTE_PARTS = 8
ROUTE_LINKS = 23

LAYERS = [
    Layer(True, ["Y1", "XT", "Y2", "T0", "Q", "N0", "T1", "P0", "KV", "N1", "T2", "P1", "N2", "T3", "P2", "N3", "T4", "P3", "N4", "Y0", "T5", "P4", "N5", "N6", "T6", "P5", "N7", "T7", "P6", "M", "P7", "YT", "O"]),
    Layer(False, ["Y2", "XT", "YT", "Q", "O", "T0", "N0", "T1", "P0", "N1", "T2", "P1", "N2", "N3", "T3", "P2", "P3", "M"]),
]


class AttentionSignals:

    def __init__(self, sem, l):
        self.mv_ready = sem(f"mv_ready{l}")
        self.rstd_chain = sem(f"rstd_chain{l}")
        self.rstd_ready = sem(f"rstd_ready{l}")
        self.ln_chain = sem(f"ln_chain{l}")
        self.xn_ready = sem(f"xn_ready{l}")
        self.misc_full = sem(f"misc_full{l}")
        self.misc_free = sem(f"misc_free{l}")
        self.cut_chain = sem(f"cut_chain{l}")
        self.q_cut = sem(f"q_cut{l}")
        self.k_cut = sem(f"k_cut{l}")
        self.stack_written = sem(f"stack_written{l}")
        self.stack_in = sem(f"stack_in{l}")
        self.m_written = sem(f"m_written{l}")
        self.m_in = sem(f"m_in{l}")
        self.nat_full = [sem(f"nat_full{l}_{k}") for k in range(2)]
        self.nat_free = [sem(f"nat_free{l}_{k}") for k in range(2)]
        self.tr_full = [sem(f"tr_full{l}_{k}") for k in range(2)]
        self.probs = [sem(f"probs{l}_{k}") for k in range(2)]
        self.m_chain = sem(f"m_chain{l}")
        self.m_cut = sem(f"m_cut{l}")
        self.pv_done = sem(f"pv_done{l}")
        self.yu_ready = sem(f"yu_ready{l}")
        self.vx_ready = sem(f"vx_ready{l}")
        self.xb_ready = sem(f"xb_ready{l}")
        self.y_chain = sem(f"y_chain{l}")
        self.y_ready = sem(f"y_ready{l}")


class ExpertSignals:

    def __init__(self, sem):
        self.mv_ready = sem("f_mv_ready")
        self.rstd_chain = sem("f_rstd_chain")
        self.rstd_ready = sem("f_rstd_ready")
        self.ln_chain = sem("f_ln_chain")
        self.xn_ready = sem("f_xn_ready")
        self.misc_full = sem("f_misc_full")
        self.misc_free = sem("f_misc_free")
        self.wt_zeroed = sem("f_wt_zeroed")
        self.r_chain = sem("f_r_chain")
        self.w_cut = sem("f_w_cut")
        self.gate_full = sem("f_gate_full")
        self.up_full = sem("f_up_full")
        self.wb_full = sem("f_wb_full")
        self.s_ready = sem("f_s_ready")
        self.t_ready = sem("f_t_ready")
        self.h_ready = sem("f_h_ready")
        self.h_used = sem("f_h_used")
        self.yt_ready = sem("f_yt_ready")


class SparseSignals:

    def __init__(self, sem):
        self.ln_chain = sem("s_ln_chain")
        self.mv_ready = sem("s_mv_ready")
        self.rstd_chain = sem("s_rstd_chain")
        self.rstd_ready = sem("s_rstd_ready")
        self.xn_ready = sem("s_xn_ready")
        self.xt_full = sem("s_xt_full")
        self.xt_copied = sem("s_xt_copied")
        self.routed = sem("s_routed")
        self.shifted = sem("s_shifted")
        self.exps = sem("s_exps")
        self.chain = sem("s_chain")
        self.sel_ready = sem("s_sel_ready")
        self.rank_ready = sem("s_rank_ready")
        self.te_ready = sem("s_te_ready")
        self.pos_ready = sem("s_pos_ready")
        self.xs_zeroed = sem("s_xs_zeroed")
        self.yu_zeroed = sem("s_yu_zeroed")
        self.scattered = sem("s_scattered")
        self.x_taken = sem("s_x_taken")
        self.x_copied = sem("s_x_copied")
        self.gate_full = sem("s_gate_full")
        self.up_full = sem("s_up_full")
        self.s_ready = sem("s_s_ready")
        self.h_ready = sem("s_h_ready")
        self.ht_full = sem("s_ht_full")
        self.ht_copied = sem("s_ht_copied")
        self.y_full = sem("s_y_full")
        self.y_ready = sem("s_y_ready")
        self.g_used = sem("s_g_used")
        self.tile_in = [sem(f"s_tile_in{k}") for k in range(NBUF)]
        self.ys_written = [sem(f"s_ys_written{k}") for k in range(NBUF)]
        self.g_in = [sem(f"s_g_in{k}") for k in range(GBUF)]


def at_least(eng, sem, value):
    if isinstance(value, int) and value <= 0:
        return
    eng.wait_ge(sem, value)


def steps(eng, step):
    for s in range(4):
        step(s, s % 2, s < B, 0 <= s - 1 < B, 0 <= s - 2 < B, 0 <= s - 3 < B)
    with eng.Fori(0, (B - 4) // 2) as g:
        for k in range(2):
            step(g * 2 + (4 + k), k, True, True, True, True)
    for s in (B, B + 1, B + 2):
        step(s, s % 2, False, s - 1 < B, s - 2 < B, True)


def chunks(eng, chunk):
    chunk(0, 0, True)
    with eng.Fori(0, (NCH - 2) // 2) as g:
        for k in range(2):
            chunk(g * 2 + (1 + k), (1 + k) % 2, True)
    chunk(NCH - 1, (NCH - 1) % 2, False)


def bass_two_layers(nc, t, out):
    ctx = ExitStack()
    with ctx:
        def sb(name, shape, dt=F32):
            return ctx.enter_context(nc.sbuf_tensor(name, shape, dt))

        def sem(name):
            return ctx.enter_context(nc.semaphore(name))

        identf, identb = sb("identf", [P, P]), sb("identb", [P, P], BF)
        mask_nat, mask_tr = sb("mask_nat", [P, 2, P], BF), sb("mask_tr", [P, 2, P], BF)
        keep = sb("keep", [P, 2])
        lower = sb("lower", [P, G0, G0])
        sel0 = sb("sel0", [P, U0 - 1, P], BF)
        bias_in = sb("bias_in", [P, 8])
        bias_kz = sb("bias_kz", [P, 2, 2])
        bias_y = sb("bias_y", [P, 2])
        bp_row = sb("bp_row", [P, P])
        w_att = [sb("w_att0", [P, 5, P]), sb("w_att1", [P, 2, P])]
        w_ctx = sb("w_ctx", [CC, 2, 2, P])
        neg_half = sb("neg_half", [P, CT])
        w_router0, w_router1 = sb("w_router0", [P, E0]), sb("w_router1", [P, E1])
        router_bias = sb("router_bias", [P, E0])
        w_gate0, w_up0 = (sb(n, [P, U0, P]) for n in ("w_gate0", "w_up0"))

        X = sb("X", [P, NT, C])
        region5 = sb("region5", [P, NJ * NCTX])
        KC = region5[:, :].bitcast(BF).rearrange("p (j n) -> p j n", j=NJ)
        region4 = sb("region4", [P, U0 * P])
        VC = [region4[:, 0:B * P].rearrange("p (b c) -> p b c", b=B), sb("VC1", [P, B, P])]
        w_down0 = region4[:, :].rearrange("p (u c) -> p u c", u=U0)

        region1 = sb("region1", [P, 12288])
        KZ = [region1[:, 2048 * k:2048 * (k + 1)].bitcast(BF).rearrange("p (j s t) -> p j s t", j=NJ, s=2)
              for k in range(2)]
        ctx_t = region1[:, 4096:5120]
        kc_f = region1[:, 5120:7168]
        kc_r = region1[:, 7168:9216]
        kc_parts = region1[:, 9216:12288].bitcast(BF).rearrange("p (r n) -> p r n", r=3)

        region2 = sb("region2", [P, 6656])
        QS = [region2[:, 2048 * k:2048 * (k + 1)].bitcast(BF) for k in range(2)]
        zeros_m = region2[0:MROWS, 4096:6144].bitcast(BF)
        PR = region2[:, 4096:6144].rearrange("p (r k n) -> p r k n", r=2, k=2)
        hid_s = region2[:, 0:1024].rearrange("p (r n) -> p r n", r=2)
        hid_t = region2[:, 1024:2048].rearrange("p (r n) -> p r n", r=2)
        hid_h = region2[:, 2048:3072].rearrange("p (r n) -> p r n", r=2)
        xt_f = region2[:, 4096:5120].rearrange("p (r n) -> p r n", r=2)
        yt_f = region2[:, 5120:5632]
        wt_f = [region2[:, 5632 + 256 * k:5888 + 256 * k].bitcast(BF) for k in range(2)]
        xn_f = region2[:, 6144:6656].rearrange("p (t n) -> p t n", t=CT)

        stats = sb("stats", [P, CT, 6])
        mv = sb("mv", [P, CT, 2])
        var_e, rstd = sb("var_e", [P, CT]), sb("rstd", [P, CT])
        xn = sb("xn", [P, 2, C])
        xt = [sb(f"xt{k}", [P, T]) for k in range(2)]
        qf, kf, rest = (sb(n, [P, 2 * T]) for n in ("qf", "kf", "rest"))
        q_parts, k_parts = sb("q_parts", [P, 3, 2 * T], BF), sb("k_parts", [P, 3, 2 * T], BF)
        region3 = sb("region3", [P, 2048])
        V = [region3[:, 1024 * k:1024 * k + 1024].rearrange("p (k h n) -> p k h n", k=2, n=32) for k in range(2)]
        VX = [sb(f"VX{k}", [P, NJ, 32]) for k in range(2)]
        nmax, nmax_r = sb("nmax", [P, 4, 2, NJ]), sb("nmax_r", [P, 4, 2, NJ])
        nmax_p = sb("nmax_p", [P, 4, 2, 3, NJ], BF)
        mt = sb("mt", [48, 2 * T], BF)
        yu = sb("yu", [P, 2 * T])
        den = sb("den", [P, 32])
        y_own, y_ctx, y_all = sb("y_own", [P, 2, P]), sb("y_ctx", [P, 2, P]), sb("y_all", [P, 2, P])
        yt = sb("yt", [P, T])
        xb = sb("xb", [P, 2, C])

        ex, sig, biased, wsel, wgt, wrest, top_g = (
            region3[:, 128 * k:128 * k + 128].rearrange("p (t e) -> p t e", e=E0 if k < 6 else 8) for k in range(7))
        w_parts = region3[:, 896:1088].bitcast(BF).rearrange("p (t e) -> p t e", t=CT)
        gs = sb("gs", [P, CT, G0])
        cmp_a, cmp_b = sb("cmp_a", [P, CT, G0, G0]), sb("cmp_b", [P, CT, G0, G0])
        rank, gmask = sb("rank", [P, CT, G0]), sb("gmask", [P, CT, G0])
        cand0, mark0 = sb("cand0", [P, CT, E0 + 8 - K0]), sb("mark0", [P, CT, E0 + 8 - K0])
        top, take0 = sb("top", [P, CT, 8]), sb("take0", [P, CT, 8])
        wsum, winv = sb("wsum", [P, CT]), sb("winv", [P, CT])

        tri, ones = sb("tri", [P, P], BF), sb("ones", [P, P], BF)
        route_c = sb("route_c", [P, E1 + NT + E1 * E1 + ST])
        desc = route_c[:, 0:E1]
        times_p = route_c[:, E1:E1 + NT]
        upto = route_c[:, E1 + NT:E1 + NT + E1 * E1].rearrange("p (a b) -> p a b", a=E1)
        tile_no = route_c[:, E1 + NT + E1 * E1:]
        w_gu_s = region1[:, 0:8192].rearrange("p (e a n) -> p e a n", e=E1, a=2)
        w_dn_s = region1[:, 8192:12288].rearrange("p (e k n) -> p e k n", e=E1, k=4)
        xn_all = region5[:, 0:4096].rearrange("p (t c) -> p t c", t=NT)
        g_buf = region5[:, 4096:5120].rearrange("p (k c) -> p k c", k=GBUF)
        tile_x = region5[:, 5120:5632].rearrange("p (k c) -> p k c", k=NBUF)
        tile_xt = region5[:, 5632:5888].rearrange("p (k c) -> p k c", k=2)
        tile_y = region5[:, 5888:6400].rearrange("p (k c) -> p k c", k=NBUF)
        tile_ht = region5[:, 6400:7424].rearrange("p (k n) -> p k n", k=2)
        shifted, ex_s, prob, prob2, eq, key, first, second = (
            region4[:, 256 * k:256 * k + 256].rearrange("p (t e) -> p t e", e=E1) for k in range(8))
        chosen = (first, second)
        best = region4[:, 2048:2112].rearrange("p (n t) -> p n t", n=2)
        best_key = region4[:, 2112:2144]
        wsum_s = region4[:, 2144:2176]
        sel = region3[:, 0:128].bitcast(BF)
        sel_sum = region3[:, 128:132].bitcast(BF)
        slot_s = region3[:, 136:392].rearrange("p (t e) -> p t e", e=E1)
        slot_of = region3[:, 392:904].rearrange("p (n t e) -> p n t e", n=2, e=E1)
        cmp_s = region3[:, 904:904 + ST * E1]
        tiles_of, tiles_to, start_s = (region3[:, 1480 + 8 * k:1488 + 8 * k] for k in range(3))
        tile_e = region3[:, 1504:1504 + ST]
        pos_f = region3[:, 1576:1640]
        winv_s = region3[:, 1640:1672]
        weight = region3[:, 1672:1736].rearrange("p (n t) -> p n t", n=2)
        stats_s = region3[:, 1736:1928].rearrange("p (t n) -> p t n", t=NT)
        mv_s = sb("mv_s", [P, NT, 2])
        var_s, rstd_s, half_s = (region3[:, 1928 + 32 * k:1960 + 32 * k] for k in range(3))
        expert_of = sb("expert_of", [P, ST], I32)
        slot_no = sb("slot_no", [P, 2 * NT], U32)

        bank = [ctx.enter_context(nc.psum_tensor(f"bank{i}", [P, 512], F32)) for i in range(8)]
        nat_ps, tr_ps, pv_ps, misc = bank[0:2], bank[2:4], bank[4:7], bank[7]
        gate_ps, up_ps, wb_ps, y_ps = bank[0:2], bank[2:4], bank[4:6], bank[6]

        q_scr = [[nc.dram_tensor(f"q_scr{l}_{k}", [SROWS + MROWS, NJ * LAYERS[l].tw], BF).ap() for k in range(2)]
                 for l in range(2)]
        k_scr = [nc.dram_tensor(f"k_scr{k}", [SROWS, NJ * 2 * T], BF).ap() for k in range(2)]
        kc_scr = [nc.dram_tensor(f"kc_scr{k}", [SROWS, NJ * 2 * NCTX], BF).ap() for k in range(2)]
        m_scr = [nc.dram_tensor(f"m_scr{l}", [MROWS, NJ * LAYERS[l].tw], BF).ap() for l in range(2)]

        xs_dram = nc.dram_tensor("xs_dram", [ST * P, C], F32).ap()
        ys_dram = nc.dram_tensor("ys_dram", [ST * P, C], F32).ap()

        consts_in, x_in, gu0_in, w1_in = sem("consts_in"), sem("x_in"), sem("gu0_in"), sem("w1_in")
        ctx_in = sem("ctx_in")
        set_up, bias_done, zeros_ready, scr_zeroed = (
            sem("set_up"), sem("bias_done"), sem("zeros_ready"), sem("scr_zeroed"))
        kc_full, kc_flat, kc_chain, kc_cut, kc_written, kc_in = (
            sem(n) for n in ("kc_full", "kc_flat", "kc_chain", "kc_cut", "kc_written", "kc_in"))
        vc_full, vc_free = sem("vc_full"), sem("vc_free")
        tails_in = sem("tails_in")
        out_done, apart, stacks_zeroed = sem("out_done"), sem("apart"), sem("stacks_zeroed")

        A = [AttentionSignals(sem, l) for l in range(2)]
        F = ExpertSignals(sem)
        S = SparseSignals(sem)

        def wait_alone(eng, sem, value):
            if isinstance(value, int):
                at_least(eng, sem, value)
                return
            eng.wait_ge(sem, value)
            eng.sem_inc(apart, 1)

        def stack_in_cols(buf, tw):
            return buf[:, 0:NJ * tw].rearrange("p (j t) -> p j t", j=NJ)

        block = ctx.enter_context(nc.Block())

        @block.sync
        def _(sp):
            n = 0
            for dst, name in ((identf[:, :], "c_identf"), (identb[:, :], "c_identb"), (keep[:, :], "c_keep"),
                              (mask_nat[:, :, :], "c_mask_nat"), (mask_tr[:, :, :], "c_mask_tr"),
                              (lower[:, :, :], "c_lower"), (sel0[:, :, :], "c_sel0"), (tri[:, :], "c_tri"), (ones[:, :], "c_ones"), (route_c[:, :], "c_route"),
                              (bias_in[:, 0:6], "biases"), (w_att[0][:, :, :], "w_att0"),
                              (w_att[1][:, :, :], "w_att1"), (w_ctx[:, :, :, :], "w_ctx"),
                              (w_router0[:, :], "w_router0"), (w_router1[:, :], "w_router1")):
                sp.dma_start(dst, t[name]).then_inc(consts_in, 16)
            sp.dma_start(bp_row[:, :], t["bp"].partition_broadcast(P)).then_inc(consts_in, 16)
            sp.dma_start(router_bias[:, :], t["router_bias"].partition_broadcast(P)).then_inc(consts_in, 16)
            sp.dma_start(ctx_t[0:CC, :], t["ctx"]).then_inc(ctx_in, 16)
            sp.dma_start(X[:, :, :], t["x"]).then_inc(x_in, 16)
            for k in range(2):
                sp.dma_start(KZ[k][SROWS:P, :, :, :].rearrange("p j s t -> p j (s t)"),
                             t["c_tail"].unsqueeze(1).broadcast_to([P - SROWS, NJ, 2 * T])).then_inc(tails_in, 16)
                sp.dma_start(QS[k][SROWS:P, :], t["c_zero"]).then_inc(tails_in, 16)
            sp.dma_start(KC[SROWS:P, :, :].rearrange("p j (b n) -> p (j b) n", b=B),
                         t["c_tail_ctx"].unsqueeze(1).broadcast_to([P - SROWS, NJ * B, 2 * TC]))\
              .then_inc(tails_in, 16)
            sp.wait_ge(zeros_ready, 1)
            for l in range(2):
                for k in range(2):
                    sp.dma_start(q_scr[l][k][SROWS:SROWS + MROWS, :], zeros_m[:, 0:NJ * LAYERS[l].tw])\
                      .then_inc(scr_zeroed, 16)
            for l in range(2):
                sp.wait_ge(kc_cut, l + 1)
                rows = kc_scr[l].rearrange("(r q) (j n) -> (q j) r n", r=SLOTS, j=NJ)
                for a, b, k in ((0, 3, 3), (3, 5, 2), (5, 6, 1)):
                    sp.dma_start(rows[:, a:b, :], kc_parts[:, 0:k, :]).then_inc(kc_written, 16)
                if l == 0:
                    sp.wait_ge(kc_written, 48)
                    sp.dma_start(KC[0:SROWS, :, :].rearrange("p j n -> p (j n)"), kc_scr[l]).then_inc(kc_in, 16)
            sp.dma_start(w_gate0[:, :, :], t["w_gate0"]).then_inc(gu0_in, 16)
            sp.dma_start(w_up0[:, :, :], t["w_up0"]).then_inc(gu0_in, 16)
            for l in range(2):
                lay, a = LAYERS[l], A[l]
                tw = lay.tw
                if l == 1:
                    sp.wait_ge(A[0].misc_free, LAYERS[0].total)
                    sp.dma_start(w_down0, t["w_down0"]).then_inc(gu0_in, 16)
                    sp.wait_ge(S.yu_zeroed, 1)
                    sp.dma_start(xs_dram.rearrange("(a p) c -> p a c", p=P),
                                 yu[:, 0:C].unsqueeze(1).broadcast_to([P, ST, C])).then_inc(S.xs_zeroed, 16)
                    sp.wait_ge(kc_written, 96)
                    sp.dma_start(KC[0:SROWS, :, :].rearrange("p j n -> p (j n)"), kc_scr[l]).then_inc(kc_in, 16)
                else:
                    sp.wait_ge(scr_zeroed, 64)
                    sp.wait_ge(tails_in, 80)
                if l == 1:
                    sp.dma_start(w_gu_s, t["w_gu1"]).then_inc(w1_in, 16)
                    sp.dma_start(w_dn_s, t["w_dn1"]).then_inc(w1_in, 16)
                    sp.wait_ge(F.misc_free, F_USES)
                    sp.wait_ge(stacks_zeroed, 2)
                per_w = 96 if lay.own else 48
                per_r = 32 if lay.own else 16

                def step(s, par, prep, nat, trans, tail):
                    if prep:
                        wait_alone(sp, a.stack_in, (s - 1) * per_r)
                        wait_alone(sp, a.q_cut, s + 1)
                        rows = q_scr[l][par][0:SROWS, :].rearrange("(r q) (j n) -> (q j) r n", r=SLOTS, j=NJ)
                        for lo, hi, k in ((0, 3, 0), (3, 5, 1), (5, 6, 2)):
                            src = q_parts[:, k:k + 1, 0:tw].broadcast_to([P, hi - lo, tw])
                            sp.dma_start(rows[:, lo:hi, :], src).then_inc(a.stack_written, 16)
                        if lay.own:
                            wait_alone(sp, a.k_cut, s + 1)
                            rows = k_scr[par].rearrange("(r q) (j n) -> (q j) r n", r=SLOTS, j=NJ)
                            for lo, hi, k in ((0, 3, 3), (3, 5, 2), (5, 6, 1)):
                                sp.dma_start(rows[:, lo:hi, :], k_parts[:, 0:k, :]).then_inc(a.stack_written, 16)
                    def stacks_in():
                        wait_alone(sp, a.stack_written, (s + 1) * per_w)
                        for full in a.tr_full:
                            wait_alone(sp, full, (s - 1) * (lay.units if lay.own else lay.units // 2))
                        sp.dma_start(QS[par][0:SROWS + MROWS, 0:NJ * tw], q_scr[l][par])\
                          .then_inc(a.stack_in, 16)
                        if lay.own:
                            sp.dma_start(KZ[par][0:SROWS, :, :, :].rearrange("p j s t -> p (j s t)"), k_scr[par])\
                              .then_inc(a.stack_in, 16)

                    if nat:
                        wait_alone(sp, a.misc_free, lay.before(s, "M") + 1)
                        wait_alone(sp, a.m_in, (s - 1) * 16)
                        rows = m_scr[l].rearrange("m (j n) -> (m j) n", j=NJ)
                        sp.dma_start(rows, mt[:, 0:tw]).then_inc(a.m_written, 16)
                        wait_alone(sp, a.m_written, s * 16)
                        sp.dma_start(QS[1 - par][SROWS:SROWS + MROWS, 0:NJ * tw], m_scr[l])\
                          .then_inc(a.m_in, 16)
                    if prep:
                        stacks_in()
                steps(sp, step)
            sp.wait_ge(S.scattered, 16 * 2 * NT)
            for i in range(NBUF):
                sp.dma_start(tile_x[:, i, :], xs_dram[P * i:P * i + P, :]).then_inc(S.tile_in[i], 16)

            def tile(i, q, more):
                wait_alone(sp, S.y_ready, i + 1)
                sp.dma_start(ys_dram[bass.ds(i * P, P), :], tile_y[:, q, :]).then_inc(S.ys_written[q], 16)
                if more:
                    wait_alone(sp, S.x_taken, i + 1)
                    sp.dma_start(tile_x[:, q, :], xs_dram[bass.ds((i + NBUF) * P, P), :]).then_inc(S.tile_in[q], 16)

            with sp.Fori(0, (ST - NBUF) // NBUF) as g:
                for q in range(NBUF):
                    tile(g * NBUF + q, q, True)
            for q in range(NBUF):
                tile(ST - NBUF + q, q, False)
            for c in range(4):
                sp.wait_ge(S.g_used, 2 * NT // 4 * (c + 1))
                sp.dma_start(out[:, 8 * c:8 * c + 8, :], X[:, 8 * c:8 * c + 8, :]).then_inc(out_done, 16)
            sp.wait_ge(out_done, 64)

        @block.gpsimd
        def _(pool):
            pool.memset(zeros_m[:, :], 0.0).then_inc(zeros_ready, 1)
            pool.wait_ge(zeros_ready, 1)
            done = [0]

            def fill(dst, value):
                pool.memset(dst, value).then_inc(set_up, 1)
                done[0] += 1
                pool.wait_ge(set_up, done[0])

            fill(neg_half[:, :], -0.5)
            for k in range(2):
                fill(V[k][:, :, :, :], 0.0)
                fill(VX[k][:, :, :], 0.0)
                fill(V[k][:, :, :, D:D + 1], 1.0)
                fill(VX[k][0:64, :, D:D + 1], 1.0)
                fill(VX[k][64:P, :, 2 * D + 1:2 * D + 2], 1.0)
            fill(cand0[:, :, E0:], -HUGE)
            fill(take0[:, :, K0:], -HUGE)
            assert done[0] == SET_UP
            pool.wait_ge(x_in, 16)

            def rsqrt(f, i, n):
                wait_alone(pool, f.mv_ready, i + 1)
                pool.tensor_scalar(var_e[:, 0:n], mv[:, 0:n, 1], EPS, None, ALU.add).then_inc(f.rstd_chain, 1)
                pool.wait_ge(f.rstd_chain, i + 1)
                pool.tensor_tensor(rstd[:, 0:n], var_e[:, 0:n], neg_half[:, 0:n], ALU.pow).then_inc(f.rstd_ready, 1)

            for l in range(2):
                lay, a = LAYERS[l], A[l]
                tw = lay.tw
                per = 6 if lay.own else 3
                if l == 1:
                    pool.wait_ge(F.misc_free, F_USES)
                    for k in range(2):
                        pool.memset(QS[k][SROWS:P, 0:NJ * tw], 0.0).then_inc(stacks_zeroed, 1)
                        pool.wait_ge(stacks_zeroed, k + 1)

                def cut(src, parts, n, base, done):
                    pool.tensor_copy(parts[:, 0, 0:n], src[:, 0:n]).then_inc(a.cut_chain, 1)
                    pool.wait_ge(a.cut_chain, base + 1)
                    pool.tensor_tensor(rest[:, 0:n], src[:, 0:n], parts[:, 0, 0:n], ALU.subtract).then_inc(a.cut_chain, 1)
                    wait_alone(pool, a.cut_chain, base + 2)
                    pool.tensor_copy(parts[:, 1, 0:n], rest[:, 0:n]).then_inc(a.cut_chain, 1)
                    pool.wait_ge(a.cut_chain, base + 3)
                    pool.tensor_tensor(parts[:, 2, 0:n], rest[:, 0:n], parts[:, 1, 0:n], ALU.subtract).then_inc(done, 1)

                def step(s, par, prep, nat, trans, tail):
                    if prep:
                        rsqrt(a, s, 2)
                        wait_alone(pool, a.misc_free, lay.before(s, "Q") + 1)
                        wait_alone(pool, a.stack_written, s * (96 if lay.own else 48))
                        cut(qf, q_parts, tw, s * per, a.q_cut)
                        if lay.own:
                            wait_alone(pool, a.misc_free, lay.before(s, "KV") + 1)
                            cut(kf, k_parts, 2 * T, s * per + 3, a.k_cut)
                    if nat:
                        b = s - 1
                        wait_alone(pool, a.pv_done, (s - 2) * lay.units)
                        pool.wait_ge(vc_free, 8)
                        if prep:
                            wait_alone(pool, a.k_cut if lay.own else a.q_cut, s + 1)
                        elif lay.own:
                            wait_alone(pool, a.xb_ready, (s - 2) * 2)
                        src = VC[l][:, bass.ds(b, 1), :].rearrange("p b (j s d) -> p (b j) s d", s=2, d=D)
                        pool.tensor_copy(VX[1 - par][0:64, :, 0:D], src[0:64, :, 0, :]).then_inc(a.vx_ready, 1)
                        wait_alone(pool, a.vx_ready, b * 2 + 1)
                        pool.tensor_copy(VX[1 - par][64:P, :, D + 1:2 * D + 1], src[64:P, :, 1, :]).then_inc(a.vx_ready, 1)
                        wait_alone(pool, a.vx_ready, b * 2 + 2)
                    if trans and lay.own:
                        b = s - 2
                        if not isinstance(s, int) or b > 0:
                            pool.wait_ge(a.misc_free, lay.before(s, "O") + 1)
                        for i in range(2):
                            pool.tensor_tensor(xb[:, i, :], X[:, bass.ds(b * 2 + i, 1), :].rearrange("p a c -> p (a c)"),
                                               bp_row[:, :], ALU.add).then_inc(a.xb_ready, 1)

                steps(pool, step)
                pool.wait_ge(a.misc_free, lay.total)
                if l == 0:
                    pool.memset(yu[:, :], 0.0).then_inc(S.yu_zeroed, 1)
                    pool.wait_ge(S.yu_zeroed, 1)
                    with pool.Fori(0, NCH) as c:
                        rsqrt(F, c, CT)

            pool.memset(half_s, -0.5).then_inc(S.rstd_chain, 1)
            pool.wait_ge(S.mv_ready, 1)
            pool.tensor_scalar(var_s, mv_s[:, :, 1], EPS, None, ALU.add).then_inc(S.rstd_chain, 1)
            pool.wait_ge(S.rstd_chain, 2)
            pool.tensor_tensor(rstd_s, var_s, half_s, ALU.pow).then_inc(S.rstd_ready, 1)
            pool.wait_ge(S.xs_zeroed, 16)
            pool.wait_ge(S.xn_ready, NCH)
            pool.wait_ge(S.pos_ready, 1)
            for i in range(NT):
                for n in range(2):
                    at = bass.IndirectOffsetOnAxis(ap=slot_no[:, n * NT + i:n * NT + i + 1], axis=0)
                    pool.indirect_dma_start(out=xs_dram, out_offset=at, in_=xn_all[:, i, :], in_offset=None)\
                        .then_inc(S.scattered, 16)
            for q in range(NBUF):
                pool.wait_ge(S.ys_written[q], 16 * (ST // NBUF))
            for i in range(NT):
                for n in range(2):
                    j = 2 * i + n
                    at_least(pool, S.g_used, j - GBUF + 1)
                    at = bass.IndirectOffsetOnAxis(ap=slot_no[:, n * NT + i:n * NT + i + 1], axis=0)
                    pool.indirect_dma_start(out=g_buf[:, j % GBUF, :], out_offset=None, in_=ys_dram, in_offset=at)\
                        .then_inc(S.g_in[j % GBUF], 16)

        @block.scalar
        def _(act):
            act.wait_ge(consts_in, CONSTS)
            act.wait_ge(bias_done, 4)
            for l in range(2):
                act.wait_ge(kc_full, l + 1)
                if l == 1:
                    act.wait_ge(kc_cut, 1)
                for s in range(2):
                    for h in range(2):
                        bias = bias_kz[:, 1, s:s + 1] if l == 0 else 0.0
                        o = kc_f[:, 1024 * h:1024 * h + 1024].rearrange("p (b s t) -> p b s t", s=2, t=TC)
                        act.activation(o[:, :, s, :], nat_ps[h][:, :].rearrange("p (b t) -> p b t", t=TC), ACT.Identity, bias=bias,
                                       scale=keep[:, s:s + 1]).then_inc(kc_flat, 1)
                for r in range(4):
                    act.wait_ge(vc_full, 4 * l + r + 1)
                    act.activation(VC[l][:, 4 * r:4 * r + 4, :].rearrange("p b c -> p (b c)"),
                                   [*tr_ps, *pv_ps[0:2]][r][:, :], ACT.Copy).then_inc(vc_free, 1)

            for l in range(2):
                lay, a = LAYERS[l], A[l]
                tw = lay.tw
                if l == 1:
                    act.wait_ge(F.misc_free, F_USES)
                    act.wait_ge(S.xs_zeroed, 16)
                act.wait_ge(set_up, SET_UP)

                def step(s, par, prep, nat, trans, tail):
                    for e in lay.order:
                        if not lay.live(e, prep, nat, trans, tail):
                            continue
                        if e in lay.uses and e not in ("O", "Y0", "Y1", "Y2"):
                            act.wait_ge(a.misc_full, lay.before(s, e) + 1)
                        if e[0] == "T":
                            j = int(e[1:])
                            n = (s - 2) * lay.units + j
                            if lay.own:
                                at_least(act, a.pv_done, n - 1)
                                for k in range(2):
                                    act.wait_ge(a.tr_full[k], n + 1)
                                    act.activation(PR[:, j % 2, k, :], tr_ps[k][:, :], ACT.Exp, scale=SCALE)\
                                       .then_inc(a.probs[k], 1)
                            else:
                                at_least(act, a.pv_done, n - 3)
                                k = j % 2
                                act.wait_ge(a.tr_full[k], (s - 2) * 2 + (j // 2 + 1))
                                act.activation(PR[:, j // 2, k, :], tr_ps[k][:, :], ACT.Exp, scale=SCALE)\
                                   .then_inc(a.probs[k], 1)
                        elif e == "XT":
                            act.activation(xt[par][:, :], misc[:, 0:T], ACT.Copy).then_inc(a.misc_free, 1)
                        elif e == "Q":
                            at_least(act, a.q_cut, s)
                            if lay.own:
                                act.activation(qf[:, 0:T], misc[:, 0:T], ACT.Identity, bias=bias_in[:, 0:1])
                                act.activation(qf[:, T:2 * T], misc[:, T:2 * T], ACT.Identity, bias=bias_in[:, 1:2])\
                                   .then_inc(a.misc_free, 1)
                            else:
                                act.activation(qf[:, 0:T], misc[:, 0:T], ACT.Copy).then_inc(a.misc_free, 1)
                        elif e == "KV":
                            last = None
                            if prep:
                                at_least(act, a.k_cut, s)
                                for i in range(2):
                                    last = act.activation(kf[:, T * i:T * i + T], misc[:, 0:T], ACT.Identity,
                                                          bias=bias_kz[:, 0, i:i + 1], scale=keep[:, i:i + 1])
                            if nat:
                                at_least(act, a.pv_done, (s - 2) * lay.units)
                                last = act.activation(V[1 - par][:, :, :, 0:D],
                                                      misc[:, T:2 * T].rearrange("p (k h d) -> p k h d", k=2, d=D), ACT.Copy)
                            last.then_inc(a.misc_free, 1)
                        elif e == "M":
                            at_least(act, a.m_written, (s - 1) * 16)
                            act.activation(mt[:, 0:tw], misc[0:48, :].bitcast(BF)[:, 0:tw], ACT.Copy).then_inc(a.misc_free, 1)
                        elif e in ("Y0", "Y1", "Y2"):
                            k = int(e[1])
                            act.wait_ge(a.pv_done, (s - 2) * lay.units + (4 if e == "Y0" else 0))
                            if e == "Y1":
                                act.wait_ge(a.misc_full, lay.before(s - 1, "Y0") + 1)
                            elif e == "Y2" and lay.own:
                                act.wait_ge(a.misc_full, lay.before(s, "Y1") + 1)
                            act.activation(yu[:, :], pv_ps[k][:, :], ACT.Copy).then_inc(a.yu_ready, 1)
                        elif e == "YT":
                            act.activation(yt[:, :], misc[:, 0:T], ACT.Identity, bias=bias_y[:, l:l + 1])\
                               .then_inc(a.misc_free, 1)

                steps(act, step)
                act.wait_ge(a.misc_free, lay.total)
                if l == 1:
                    break

                f, units = F, U0

                def prepare(what, par, c, used):
                    if what == "XT":
                        act.wait_ge(f.misc_full, used + 1)
                        act.activation(xt_f[:, par, :], misc[:, :], ACT.Copy).then_inc(f.misc_free, 1)
                    elif what == "R":
                        act.wait_ge(f.misc_full, used + 1)
                        act.activation(ex[:, :, :].rearrange("p t e -> p (t e)"), misc[:, 0:CT * E0], ACT.Exp,
                                       scale=-1.0).then_inc(f.misc_free, 1)
                    elif what == "W":
                        act.wait_ge(f.misc_full, used + 1)
                        n = 3 * E0
                        act.activation(wt_f[par][0:n, :], misc[0:n, :].bitcast(BF)[:, 0:CH], ACT.Copy)\
                           .then_inc(f.misc_free, 1)

                def chunk(c, par, more):
                    for u in range(units):
                        n = c * units + u
                        slot = (par * units + u) % 2
                        at_least(act, f.t_ready, n - 1)
                        act.wait_ge(f.gate_full, n + 1)
                        act.activation(hid_s[:, slot, :], gate_ps[slot][:, :], ACT.Silu).then_inc(f.s_ready, 1)
                        for what, at, use in ROUTING:
                            if at == u and more:
                                prepare(what, 1 - par, c + 1, c * 4 + use)
                    act.wait_ge(f.h_used, (c + 1) * units)
                    act.activation(yt_f, y_ps[:, :], ACT.Copy).then_inc(f.yt_ready, 1)

                act.wait_ge(f.wt_zeroed, 1)
                for i, what in enumerate(("XT", "R", "W")):
                    prepare(what, 0, 0, i)
                chunks(act, chunk)

            for c in range(NCH):
                act.wait_ge(S.xt_full, c + 1)
                at_least(act, S.routed, c - 1)
                act.activation(xt_f[:, c % 2, :], bank[c % 2][:, :], ACT.Copy).then_inc(S.xt_copied, 1)
            act.wait_ge(S.shifted, 1)
            act.activation(ex_s, shifted, ACT.Exp).then_inc(S.exps, 1)

            def copy_x(i, k):
                act.wait_ge(S.x_taken, i + 1)
                at_least(act, S.up_full, i - 1)
                act.activation(tile_xt[:, k, :], misc[:, 0:P], ACT.Copy).then_inc(S.x_copied, 1)

            def tile(i, q):
                k = q % 2
                act.wait_ge(S.gate_full, i + 1)
                at_least(act, S.h_ready, i - 1)
                act.activation(hid_s[:, k, :], gate_ps[k][:, :], ACT.Silu).then_inc(S.s_ready, 1)
                if not isinstance(i, int) or i + 1 < ST:
                    copy_x(i + 1, 1 - k)

            def copy_y(i, q):
                act.wait_ge(S.y_full, i + 1)
                if not isinstance(i, int) or i >= NBUF:
                    act.wait_ge(S.ys_written[q], ((i - q) // NBUF) * 16 if isinstance(i, int) else (i - q) * (16 // NBUF))
                act.activation(tile_y[:, q, :], y_ps[:, 0:P], ACT.Copy).then_inc(S.y_ready, 1)

            copy_x(0, 0)
            for i in range(NBUF + 1):
                tile(i, i % NBUF)
                if i:
                    copy_y(i - 1, (i - 1) % NBUF)
            with act.Fori(0, (ST - 2 * NBUF) // NBUF) as g:
                for q in range(NBUF):
                    i = g * NBUF + (NBUF + 1 + q)
                    tile(i, (q + 1) % NBUF)
                    copy_y(i - 1, q)
            for i in range(ST - NBUF + 1, ST):
                tile(i, i % NBUF)
                copy_y(i - 1, (i - 1) % NBUF)
            copy_y(ST - 1, (ST - 1) % NBUF)

        @block.vector
        def _(dve):
            dve.wait_ge(consts_in, CONSTS)
            dve.tensor_scalar(bias_kz[:, 0, :], keep[:, :], bias_in[:, 2:3], None, ALU.mult).then_inc(bias_done, 1)
            dve.tensor_scalar(bias_kz[:, 1, :], keep[:, :], bias_in[:, 3:4], None, ALU.mult).then_inc(bias_done, 1)
            dve.tensor_tensor(bias_y[:, 0:1], bias_in[:, 4:5], bias_in[:, 5:6], ALU.add).then_inc(bias_done, 1)
            dve.memset(bias_y[:, 1:2], 0.0).then_inc(bias_done, 1)
            for l in range(2):
                dve.wait_ge(kc_flat, 4 * l + 4)
                if l == 1:
                    dve.wait_ge(kc_written, 48)
                dve.tensor_copy(kc_parts[:, 0, :], kc_f).then_inc(kc_chain, 1)
                dve.wait_ge(kc_chain, 3 * l + 1)
                dve.tensor_tensor(kc_r, kc_f, kc_parts[:, 0, :], ALU.subtract).then_inc(kc_chain, 1)
                dve.wait_ge(kc_chain, 3 * l + 2)
                dve.tensor_copy(kc_parts[:, 1, :], kc_r).then_inc(kc_chain, 1)
                dve.wait_ge(kc_chain, 3 * l + 3)
                dve.tensor_tensor(kc_parts[:, 2, :], kc_r, kc_parts[:, 1, :], ALU.subtract).then_inc(kc_cut, 1)
            dve.wait_ge(x_in, 16)
            dve.wait_ge(set_up, SET_UP)

            def moments(f, i, first, n):
                at_least(dve, f.xn_ready, i)
                for k in range(n):
                    dve.bn_stats(stats[:, k, :], X[:, bass.ds(first + k, 1), :].rearrange("p a c -> p (a c)"))\
                       .then_inc(f.ln_chain, 1)
                wait_alone(dve, f.ln_chain, i * n + n)
                for k in range(n):
                    last = dve.bn_aggr(mv[:, k, :], stats[:, k, :])
                last.then_inc(f.mv_ready, 1)

            def normalize(f, i, first, n, dst, copied):
                dve.wait_ge(f.rstd_ready, i + 1)
                at_least(dve, f.misc_full, copied)
                for k in range(n):
                    last = dve.tensor_scalar(dst[:, k, :], X[:, bass.ds(first + k, 1), :].rearrange("p a c -> p (a c)"),
                                             mv[:, k, 0:1], rstd[:, k:k + 1], ALU.subtract, ALU.mult)
                last.then_inc(f.xn_ready, 1)

            for l in range(2):
                lay, a = LAYERS[l], A[l]
                kq = 2 * lay.kinds
                if l == 1:
                    dve.wait_ge(F.misc_free, F_USES)

                def step(s, par, prep, nat, trans, tail):
                    if prep:
                        moments(a, s, s * 2, 2)
                    for e in lay.order:
                        if e == "XT" and prep:
                            normalize(a, s, s * 2, 2, xn, lay.before(s - 1, "XT") + 1 if not isinstance(s, int) or s else 0)
                        if not lay.live(e, prep, nat, trans, tail):
                            continue
                        if e[0] == "N":
                            j = int(e[1:])
                            n = (s - 1) * lay.units + j
                            if j == 0:
                                at_least(dve, a.m_cut, s - 1)
                            if lay.own:
                                dve.wait_ge(a.nat_full[0], n + 1)
                                dve.tensor_reduce(nmax[:, 1, :, j], nat_ps[0][:, :].rearrange("p (s k) -> p s k", s=2),
                                                  AX.X, ALU.max, negate=True).then_inc(a.nat_free[0], 1)
                                dve.wait_ge(a.nat_full[1], n + 1)
                                dve.tensor_reduce(nmax[:, 0, :, j],
                                                  nat_ps[1][:, 0:T].rearrange("p (s k) -> p s k", s=2),
                                                  AX.X, ALU.max, negate=True)
                                dve.tensor_reduce(nmax[:, 2:4, :, j],
                                                  nat_ps[1][:, T:2 * T].rearrange("p (q s k) -> p q s k", q=2, s=2),
                                                  AX.X, ALU.max, negate=True).then_inc(a.nat_free[1], 1)
                            else:
                                dve.wait_ge(a.nat_full[j % 2], (s - 1) * 2 + (j // 2 + 1))
                                for i in range(2):
                                    last = dve.tensor_reduce(
                                        nmax[:, 0:2, :, 2 * j + i],
                                        nat_ps[j % 2][:, T * i:T * i + T].rearrange("p (q s k) -> p q s k", q=2, s=2),
                                        AX.X, ALU.max, negate=True)
                                last.then_inc(a.nat_free[j % 2], 1)
                            if j == lay.units - 1:
                                k = lay.units // 2 if not lay.own else lay.units
                                for q in range(2):
                                    dve.wait_ge(a.nat_free[q], s * k)
                                if not isinstance(s, int) or s > 1:
                                    dve.wait_ge(a.misc_full, lay.before(s - 1, "M") + 1)
                                c3 = (s - 1) * 3
                                src, rest = nmax[:, 0:kq, :, :], nmax_r[:, 0:kq, :, :]
                                dve.tensor_copy(nmax_p[:, 0:kq, :, 0, :], src).then_inc(a.m_chain, 1)
                                dve.wait_ge(a.m_chain, c3 + 1)
                                dve.tensor_tensor(rest, src, nmax_p[:, 0:kq, :, 0, :], ALU.subtract).then_inc(a.m_chain, 1)
                                dve.wait_ge(a.m_chain, c3 + 2)
                                dve.tensor_copy(nmax_p[:, 0:kq, :, 1, :], rest).then_inc(a.m_chain, 1)
                                dve.wait_ge(a.m_chain, c3 + 3)
                                dve.tensor_tensor(nmax_p[:, 0:kq, :, 2, :], rest, nmax_p[:, 0:kq, :, 1, :], ALU.subtract)\
                                   .then_inc(a.m_cut, 1)
                        elif e in ("Y0", "Y1"):
                            k = int(e[1])
                            c = (s - 2 - k) * 4 + k
                            dve.wait_ge(a.misc_full, lay.before(s, e) + 1)
                            o = misc[:, :].rearrange("p (q h n) -> p q h n", q=2, n=32)
                            inv = den[:, 0:16].rearrange("p (q h) -> p q h", q=2).unsqueeze(3)
                            dve.reciprocal(inv, o[:, :, :, D:D + 1]).then_inc(a.y_chain, 1)
                            dve.wait_ge(a.y_chain, c + 1)
                            dst = y_own[:, :, 64 * k:64 * k + 64].rearrange("p q (h d) -> p q h d", d=D)
                            dve.tensor_tensor(dst, o[:, :, :, 0:D], inv.broadcast_to([P, 2, 8, D]), ALU.mult)\
                               .then_inc(a.misc_free, 1)
                        elif e == "Y2":
                            per = 4 if lay.own else 2
                            c = (s - 3) * per + (2 if lay.own else 0)
                            dve.wait_ge(a.misc_full, lay.before(s, e) + 1)
                            dst = y_ctx if lay.own else y_all
                            o = misc[:, :].rearrange("p (q h n) -> p q h n", q=2, n=32)
                            for i in range(2):
                                inv = den[:, 16 * i:16 * i + 16].rearrange("p (q h) -> p q h", q=2).unsqueeze(3)
                                v = i * (D + 1)
                                dve.reciprocal(inv, o[:, :, :, v + D:v + D + 1]).then_inc(a.y_chain, 1)
                            dve.wait_ge(a.y_chain, c + 2)
                            for i in range(2):
                                inv = den[:, 16 * i:16 * i + 16].rearrange("p (q h) -> p q h", q=2).unsqueeze(3)
                                v = i * (D + 1)
                                dd = dst[:, :, :].rearrange("p q (h s d) -> p q h s d", s=2, d=D)[:, :, :, i, :]
                                last = dve.tensor_tensor(dd, o[:, :, :, v:v + D], inv.broadcast_to([P, 2, 8, D]), ALU.mult)
                            last.then_inc(a.misc_free, 1)
                            if lay.own:
                                dve.wait_ge(a.misc_free, lay.before(s, e) + 1)
                                dve.tensor_tensor(y_all[:, :, :], y_own[:, :, :], y_ctx[:, :, :], ALU.add)\
                                   .then_inc(a.y_ready, 1)
                        elif e == "O":
                            dve.wait_ge(a.misc_full, lay.before(s, e) + 1)
                            x2 = X[:, bass.ds((s - 3) * 2, 2), :]
                            if lay.own:
                                dve.wait_ge(a.xb_ready, (s - 2) * 2)
                            dve.tensor_tensor(x2, misc[:, 0:T].rearrange("p (i c) -> p i c", i=2),
                                              xb[:, :, :] if lay.own else x2, ALU.add).then_inc(a.misc_free, 1)

                steps(dve, step)
                dve.wait_ge(a.misc_free, lay.total)
                if l == 1:
                    break
                f, units = F, U0
                dve.wait_ge(a.misc_free, lay.total)
                for k in range(2):
                    last = dve.memset(wt_f[k], 0.0)
                last.then_inc(f.wt_zeroed, 1)
                total = ROUTE_LINKS
                links = [0]

                wait = lambda eng, sem, value: eng.wait_ge(sem, value)

                def link(c, ins, apart=False):
                    links[0] += 1
                    ins.then_inc(f.r_chain, 1)
                    (wait_alone if apart else wait)(dve, f.r_chain, c * total + links[0])

                def route(c, used, part):
                    ne, nk = E0, K0
                    cand, mark, take = cand0, mark0, take0
                    s_, w_, r_ = sig[:, :, 0:ne], wgt[:, :, 0:ne], wrest[:, :, 0:ne]
                    per = E0 // G0
                    tg = top_g[:, :, :].rearrange("p (t g) n -> p t g n", t=CT)
                    if part == 0:
                        links[0] = 0
                        if not isinstance(c, int) or c:
                            dve.wait_ge(f.w_cut, c)
                            dve.wait_ge(f.misc_full, used - 1)
                        dve.wait_ge(f.misc_free, used + 1)
                        link(c, dve.tensor_scalar(ex[:, :, :], ex[:, :, :], 1.0, None, ALU.add))
                        link(c, dve.reciprocal(s_, ex[:, :, :]))
                        bias = router_bias[:, :].unsqueeze(1).broadcast_to([P, CT, E0])
                        link(c, dve.tensor_tensor(biased[:, :, :], s_, bias, ALU.add), apart=True)
                    elif part in (1, 2):
                        half = CT * G0 // 2
                        for g in range((part - 1) * half, part * half):
                            last = dve.max(top_g[:, g, :], biased[:, g // G0, per * (g % G0):per * (g % G0) + per])
                        if part == 2:
                            link(c, last)
                            link(c, dve.tensor_tensor(gs[:, :, :].unsqueeze(3), tg[:, :, :, 0:1], tg[:, :, :, 1:2], ALU.add))
                    elif part == 3:
                        for k in range(CT):
                            other = gs[:, k, :].unsqueeze(1).broadcast_to([P, G0, G0])
                            this = gs[:, k, :].unsqueeze(2).broadcast_to([P, G0, G0])
                            dve.tensor_tensor(cmp_a[:, k, :, :], other, this, ALU.is_gt)
                            last = dve.tensor_tensor(cmp_b[:, k, :, :], other, this, ALU.is_equal)
                        link(c, last)
                        low = lower[:, :, :].rearrange("p a b -> p (a b)").unsqueeze(1).broadcast_to([P, CT, G0 * G0])
                        ca, cb = (x[:, :, :, :].rearrange("p t a b -> p t (a b)") for x in (cmp_a, cmp_b))
                        link(c, dve.tensor_tensor(cb, cb, low, ALU.mult))
                    elif part == 4:
                        ca, cb = (x[:, :, :, :].rearrange("p t a b -> p t (a b)") for x in (cmp_a, cmp_b))
                        link(c, dve.tensor_tensor(ca, ca, cb, ALU.add))
                        link(c, dve.tensor_reduce(rank[:, :, :], cmp_a[:, :, :, :], AX.X, ALU.add))
                        link(c, dve.tensor_scalar(gmask[:, :, :], rank[:, :, :], 1.5, None, ALU.is_lt))
                        for k in range(CT):
                            last = dve.tensor_tensor(cand[:, k, 0:ne].rearrange("p (g e) -> p g e", g=G0),
                                                     biased[:, k, :].rearrange("p (g e) -> p g e", g=G0),
                                                     gmask[:, k, :].unsqueeze(2).broadcast_to([P, G0, per]), ALU.mult)
                        link(c, last, apart=True)
                    elif part == 5:
                        for k in range(CT):
                            last = dve.max(top[:, k, :], cand[:, k, 0:ne])
                        link(c, last)
                        link(c, dve.tensor_copy(take[:, :, 0:nk], top[:, :, 0:nk]), apart=True)
                        for k in range(CT):
                            last = dve.match_replace(out=mark[:, k, :], in_to_replace=take[:, k, :],
                                                     in_values=cand[:, k, :], imm_value=HUGE)
                        link(c, last)
                        link(c, dve.tensor_scalar(wsel[:, :, 0:ne], mark[:, :, 0:ne], HUGE / 2, None, ALU.is_gt))
                    elif part == 6:
                        link(c, dve.tensor_tensor(w_, s_, wsel[:, :, 0:ne], ALU.mult))
                        link(c, dve.tensor_reduce(wsum[:, :], w_, AX.X, ALU.add))
                        link(c, dve.tensor_scalar(wsum[:, :], wsum[:, :], 1e-20, None, ALU.add))
                        link(c, dve.reciprocal(winv[:, :], wsum[:, :]))
                        link(c, dve.scalar_tensor_tensor(out=w_, in0=w_, scalar=ROUTE_SCALE,
                                                         in1=winv[:, :].unsqueeze(2).broadcast_to([P, CT, ne]),
                                                         op0=ALU.mult, op1=ALU.mult))
                    elif part == 7:
                        wp = w_parts[:, :, 0:3 * ne].rearrange("p t (r e) -> p t r e", r=3)
                        link(c, dve.tensor_copy(wp[:, :, 0, :], w_))
                        link(c, dve.tensor_tensor(r_, w_, wp[:, :, 0, :], ALU.subtract))
                        link(c, dve.tensor_copy(wp[:, :, 1, :], r_))
                        dve.tensor_tensor(wp[:, :, 2, :], r_, wp[:, :, 1, :], ALU.subtract).then_inc(f.w_cut, 1)
                        assert links[0] == total, links[0]

                def residual(c, used):
                    dve.wait_ge(f.misc_full, used + 1)
                    x4 = X[:, bass.ds(c * CT, CT), :]
                    dve.tensor_tensor(x4, misc[:, :].rearrange("p (t c) -> p t c", t=CT), x4, ALU.add)\
                       .then_inc(f.misc_free, 1)

                def chunk(c, par, more):
                    for u in range(units):
                        n = c * units + u
                        slot = (par * units + u) % 2
                        if u == LN_AT and more:
                            moments(f, c + 1, (c + 1) * CT, CT)
                        if u == LN_AT + 1 and more:
                            normalize(f, c + 1, (c + 1) * CT, CT, xn_f, c * 4 + (0 if not isinstance(c, int) or c else 1))
                        dve.wait_ge(f.s_ready, n + 1)
                        dve.wait_ge(f.up_full, n + 1)
                        at_least(dve, f.h_used, n - 1)
                        at_least(dve, f.h_ready, n - 1)
                        dve.tensor_tensor(hid_t[:, slot, :], hid_s[:, slot, :], up_ps[slot][:, :], ALU.mult)\
                           .then_inc(f.t_ready, 1)
                        dve.wait_ge(f.t_ready, n + 1)
                        if u < units - 1:
                            dve.wait_ge(f.wb_full, c * (units - 1) + (u + 1))
                            dve.tensor_tensor(hid_h[:, slot, :], hid_t[:, slot, :], wb_ps[u % 2][:, :], ALU.mult)\
                               .then_inc(f.h_ready, 1)
                        else:
                            dve.tensor_copy(hid_h[:, slot, :], hid_t[:, slot, :]).then_inc(f.h_ready, 1)
                        if u == Y_AT and (not isinstance(c, int) or c):
                            residual(c - 1, c * 4 + 2)
                        part = u - ROUTING[1][1]
                        if 0 <= part < ROUTE_PARTS and more:
                            route(c + 1, c * 4 + 4, part)

                moments(f, 0, 0, CT)
                normalize(f, 0, 0, CT, xn_f, 0)
                for part in range(ROUTE_PARTS):
                    route(0, 1, part)
                chunks(dve, chunk)
                residual(NCH - 1, F_USES - 1)

            for k in range(NT):
                dve.bn_stats(stats_s[:, k, :], X[:, k, :]).then_inc(S.ln_chain, 1)
            dve.wait_ge(S.ln_chain, NT)
            for k in range(NT):
                last = dve.bn_aggr(mv_s[:, k, :], stats_s[:, k, :])
            last.then_inc(S.mv_ready, 1)
            dve.wait_ge(S.rstd_ready, 1)
            for k in range(NT):
                last = dve.tensor_scalar(xn_all[:, k, :], X[:, k, :], mv_s[:, k, 0:1], rstd_s[:, k:k + 1],
                                         ALU.subtract, ALU.mult)
                if k % CT == CT - 1:
                    last.then_inc(S.xn_ready, 1)

            links = [0]

            def link(ins):
                links[0] += 1
                ins.then_inc(S.chain, 1)
                dve.wait_ge(S.chain, links[0])

            def each(x, n=E1):
                return x.unsqueeze(2).broadcast_to([P, x.shape[1], n])

            dve.wait_ge(S.routed, NCH)
            logits = bank[2][:, 0:NT * E1].rearrange("p (t e) -> p t e", e=E1)
            link(dve.tensor_reduce(wsum_s, logits, AX.X, ALU.max))
            dve.tensor_tensor(shifted, logits, each(wsum_s), ALU.subtract).then_inc(S.shifted, 1)
            dve.wait_ge(S.exps, 1)
            link(dve.tensor_reduce(wsum_s, ex_s, AX.X, ALU.add))
            link(dve.reciprocal(winv_s, wsum_s))
            link(dve.tensor_tensor(prob, ex_s, each(winv_s), ALU.mult))
            for n, src in enumerate((prob, prob2)):
                link(dve.tensor_reduce(best[:, n, :], src, AX.X, ALU.max))
                link(dve.tensor_tensor(eq, src, each(best[:, n, :]), ALU.is_equal))
                link(dve.tensor_tensor(key, eq, desc.unsqueeze(1).broadcast_to([P, NT, E1]), ALU.mult))
                link(dve.tensor_reduce(best_key, key, AX.X, ALU.max))
                link(dve.tensor_tensor(chosen[n], key, each(best_key), ALU.is_equal))
                if n == 0:
                    link(dve.scalar_tensor_tensor(out=prob2, in0=first, scalar=-4.0, in1=prob, op0=ALU.mult,
                                                  op1=ALU.add))
            sel_te = sel.rearrange("p (t e) -> p t e", e=E1)
            link(dve.tensor_tensor(sel_te, first, second, ALU.add))
            link(dve.tensor_reduce(tiles_of, sel_te.rearrange("p t e -> p e t"), AX.X, ALU.add))
            dve.tensor_copy(sel_sum, tiles_of).then_inc(S.sel_ready, 1)
            link(dve.tensor_tensor(wsum_s, best[:, 0, :], best[:, 1, :], ALU.add))
            link(dve.reciprocal(winv_s, wsum_s))
            for n in range(2):
                link(dve.tensor_tensor(weight[:, n, :], best[:, n, :], winv_s, ALU.mult))
            dve.wait_ge(S.rank_ready, 1)
            count = bank[4][:, 0:E1]
            cmp_t = cmp_s[:, 0:E1 * NT].rearrange("p (e k) -> p e k", e=E1)
            link(dve.tensor_tensor(cmp_t, each(count, NT), times_p.unsqueeze(1).broadcast_to([P, E1, NT]), ALU.is_gt))
            link(dve.tensor_reduce(tiles_of, cmp_t, AX.X, ALU.add))
            cmp_e = cmp_s[:, 0:E1 * E1].rearrange("p (a b) -> p a b", a=E1)
            link(dve.tensor_tensor(cmp_e, tiles_of.unsqueeze(1).broadcast_to([P, E1, E1]), upto, ALU.mult))
            link(dve.tensor_reduce(tiles_to, cmp_e, AX.X, ALU.add))
            link(dve.tensor_tensor(start_s, tiles_to, tiles_of, ALU.subtract))
            link(dve.tensor_scalar(start_s, start_s, float(P), None, ALU.mult))
            before = bank[3][:, 0:NT * E1].rearrange("p (t e) -> p t e", e=E1)
            link(dve.tensor_tensor(slot_s, before, start_s.unsqueeze(1).broadcast_to([P, NT, E1]), ALU.add))
            for n in range(2):
                link(dve.tensor_tensor(slot_of[:, n, :, :], slot_s, chosen[n], ALU.mult))
            link(dve.tensor_reduce(pos_f, slot_of.rearrange("p n t e -> p (n t) e"), AX.X, ALU.add))
            dve.tensor_copy(slot_no[:, :], pos_f).then_inc(S.pos_ready, 1)
            cmp_i = cmp_s.rearrange("p (i e) -> p i e", e=E1)
            link(dve.tensor_tensor(cmp_i, tiles_to.unsqueeze(1).broadcast_to([P, ST, E1]), each(tile_no), ALU.is_le))
            link(dve.tensor_reduce(tile_e, cmp_i, AX.X, ALU.add))
            dve.tensor_scalar(expert_of[:, :], tile_e, float(E1 - 1), None, ALU.min).then_inc(S.te_ready, 1)

            def copy_ht(i, k):
                dve.wait_ge(S.ht_full, i + 1)
                at_least(dve, S.y_full, i - 1)
                dve.tensor_copy(tile_ht[:, k, :], wb_ps[k][:, :]).then_inc(S.ht_copied, 1)

            def tile(i, q):
                k = q % 2
                if not isinstance(i, int) or i:
                    copy_ht(i - 1, 1 - k)
                dve.wait_ge(S.s_ready, i + 1)
                dve.wait_ge(S.up_full, i + 1)
                at_least(dve, S.ht_full, i - 1)
                dve.tensor_tensor(hid_h[:, k, :], hid_s[:, k, :], up_ps[k][:, :], ALU.mult).then_inc(S.h_ready, 1)

            for i in range(NBUF):
                tile(i, i)
            with dve.Fori(0, (ST - NBUF) // NBUF) as g:
                for q in range(NBUF):
                    tile(g * NBUF + (NBUF + q), q)
            copy_ht(ST - 1, 1)
            for i in range(NT):
                for n in range(2):
                    j = 2 * i + n
                    dve.wait_ge(S.g_in[j % GBUF], 16 * (j // GBUF + 1))
                    if n:
                        dve.wait_ge(S.g_used, j)
                    dve.scalar_tensor_tensor(out=X[:, i, :], in0=g_buf[:, j % GBUF, :], scalar=weight[:, n, i:i + 1],
                                             in1=X[:, i, :], op0=ALU.mult, op1=ALU.add).then_inc(S.g_used, 1)

        @block.tensor
        def _(pe):
            pe.wait_ge(consts_in, CONSTS)
            pe.wait_ge(ctx_in, 16)
            for l in range(2):
                if l == 1:
                    pe.wait_ge(kc_flat, 4)
                for h in range(2):
                    last = pe.matmul(nat_ps[h][:, :], w_ctx[:, l, 0, :], ctx_t[0:CC, 512 * h:512 * h + 512],
                                     start=True, stop=True)
                last.then_inc(kc_full, 1)
                for r in range(4):
                    at_least(pe, vc_free, 4 * (l - 1) + r + 1)
                    for k in range(4):
                        src = ctx_t[0:CC, TC * (4 * r + k):TC * (4 * r + k) + TC]
                        for half in range(2):
                            last = pe.matmul([*tr_ps, *pv_ps[0:2]][r][64 * half:64 * half + 64, P * k:P * k + P], src,
                                             w_ctx[:, l, 1, :], start=True, stop=True)
                    last.then_inc(vc_full, 1)

            for l in range(2):
                lay, a = LAYERS[l], A[l]
                tw, qc = lay.tw, lay.qc
                pe.wait_ge(kc_in, 16 * (l + 1))
                pe.wait_ge(tails_in, 80)
                pe.wait_ge(set_up, SET_UP)
                pe.wait_ge(vc_free, 8)
                if l == 1:
                    pe.wait_ge(F.misc_free, F_USES)
                wa = w_att[l]

                def step(s, par, prep, nat, trans, tail):
                    q_nat, q_tr = stack_in_cols(QS[1 - par], tw), stack_in_cols(QS[par], tw)
                    kz_nat, kz_tr = KZ[1 - par], KZ[par]
                    for e in lay.order:
                        if not lay.live(e, prep, nat, trans, tail):
                            continue
                        if e in lay.uses:
                            at_least(pe, a.misc_free, lay.before(s, e))
                        if e[0] == "N":
                            b, u = s - 1, int(e[1:])
                            n = b * lay.units + u
                            if u == 0:
                                pe.wait_ge(a.stack_in, s * (32 if lay.own else 16))
                            if lay.own:
                                at_least(pe, a.nat_free[0], n)
                                o = nat_ps[0][:, :].rearrange("p (s k) -> p s k", s=2)
                                pe.matmul(nat_ps[0][:, :], q_nat[:, u, P:T], kz_nat[:, u, :, :], start=True, stop=False,
                                          skip_group_check=True)
                                pe.matmul(o[:, :, P:T], identb[:, :], mask_nat[:, :, :], start=False, stop=True,
                                          skip_group_check=True).then_inc(a.nat_full[0], 1)
                                at_least(pe, a.nat_free[1], n)
                                pe.matmul(nat_ps[1][:, 0:T], q_nat[:, u, 0:P], kz_nat[:, u, :, 0:P], start=True,
                                          stop=False, skip_group_check=True)
                                pe.matmul(nat_ps[1][:, 0:T], identb[:, :], mask_nat[:, :, :], start=False, stop=True,
                                          skip_group_check=True)
                                for q in range(2):
                                    last = pe.matmul(nat_ps[1][:, T + P * q:T + P * q + P],
                                                     q_nat[:, u, qc + P * q:qc + P * q + P],
                                                     KC[:, u, bass.ds(b * 2 * TC, 2 * TC)], start=False, stop=True,
                                                     skip_group_check=True)
                                last.then_inc(a.nat_full[1], 1)
                            else:
                                k = u % 2
                                at_least(pe, a.nat_free[k], b * 2 + u // 2)
                                for i in range(2):
                                    for q in range(2):
                                        at = T * i + P * q
                                        last = pe.matmul(nat_ps[k][:, at:at + P], q_nat[:, 2 * u + i, P * q:P * q + P],
                                                         KC[:, 2 * u + i, bass.ds(b * 2 * TC, 2 * TC)], start=True, stop=True)
                                last.then_inc(a.nat_full[k], 1)
                        elif e[0] == "T":
                            b, u = s - 2, int(e[1:])
                            n = b * lay.units + u
                            if u == 0:
                                pe.wait_ge(a.m_in, (s - 1) * 16)
                            if lay.own:
                                at_least(pe, a.probs[0], n)
                                for i in range(2):
                                    pe.matmul(tr_ps[0][:, T * i:T * i + T], kz_tr[:, u, i, 0:P], q_tr[:, u, 0:T],
                                              start=(i == 0), stop=False, skip_group_check=True)
                                o = tr_ps[0][:, :].rearrange("p (s k) -> p s k", s=2)
                                pe.matmul(o[:, :, 0:P], identb[:, :], mask_tr[:, :, :], start=False, stop=True,
                                          skip_group_check=True).then_inc(a.tr_full[0], 1)
                                at_least(pe, a.probs[1], n)
                                for i in range(2):
                                    pe.matmul(tr_ps[1][:, P * i:P * i + P], kz_tr[:, u, i, P:T], q_tr[:, u, P:T],
                                              start=(i == 0), stop=False, skip_group_check=True)
                                pe.matmul(tr_ps[1][:, 0:T], identb[:, :], mask_tr[:, :, :], start=False, stop=True,
                                          skip_group_check=True)
                                pe.matmul(tr_ps[1][:, T:2 * T], KC[:, u, bass.ds(b * 2 * TC, 2 * TC)], q_tr[:, u, qc:qc + T],
                                          start=False, stop=True, skip_group_check=True).then_inc(a.tr_full[1], 1)
                            else:
                                k = u % 2
                                at_least(pe, a.probs[k], b * 2 + u // 2)
                                for i in range(2):
                                    last = pe.matmul(tr_ps[k][:, T * i:T * i + T], KC[:, 2 * u + i, bass.ds(b * 2 * TC, 2 * TC)],
                                                     q_tr[:, 2 * u + i, 0:T], start=True, stop=True)
                                last.then_inc(a.tr_full[k], 1)
                        elif e[0] == "P":
                            b, u = s - 2, int(e[1:])
                            n = b * lay.units + u
                            if u == 0:
                                pe.wait_ge(a.vx_ready, (s - 1) * 2)
                                at_least(pe, a.yu_ready, b * (3 if lay.own else 1))
                            if lay.own:
                                pe.wait_ge(a.probs[0], n + 1)
                                pe.wait_ge(a.probs[1], n + 1)
                                cols = T * ((u // 2) % 2)
                                for kb in range(2):
                                    for i in range(2):
                                        row = 32 * (2 * (u % 2) + i)
                                        pe.matmul(pv_ps[u // 4][row:row + 32, cols + P * kb:cols + T],
                                                  V[par][:, kb, 2 * u + i, :],
                                                  PR[:, u % 2, kb, (T if kb == 0 else P) * i:(T if kb == 0 else P) * (i + 1)],
                                                  start=(kb == 0), stop=(kb == 1), skip_group_check=True)
                                pairs = [(u, PR[:, u % 2, 1, T:2 * T])]
                            else:
                                pe.wait_ge(a.probs[u % 2], b * 2 + (u // 2 + 1))
                                pairs = [(2 * u + i, PR[:, u // 2, u % 2, T * i:T * i + T]) for i in range(2)]
                            for j, probs in pairs:
                                row, cols = 32 * (j % 4), T * (j // 4)
                                last = pe.matmul(pv_ps[2][row:row + 32, cols:cols + T], VX[par][:, j, :], probs,
                                                 start=True, stop=True)
                            last.then_inc(a.pv_done, 1)
                        elif e == "XT":
                            pe.wait_ge(a.xn_ready, s + 1)
                            for i in range(2):
                                last = pe.transpose(misc[:, P * i:P * i + P], xn[:, i, :], identf[:, :])
                            last.then_inc(a.misc_full, 1)
                        elif e == "Q":
                            for i in range(lay.kinds):
                                last = pe.matmul(misc[:, T * i:T * i + T], wa[:, i, :], xt[par][:, :], start=True, stop=True)
                            last.then_inc(a.misc_full, 1)
                        elif e == "KV":
                            if prep:
                                last = pe.matmul(misc[:, 0:T], wa[:, 2, :], xt[par][:, :], start=True, stop=True)
                            if nat:
                                for i in range(2):
                                    last = pe.matmul(misc[:, T + P * i:T + P * i + P], xt[1 - par][:, P * i:P * i + P],
                                                     wa[:, 3, :], start=True, stop=True)
                            last.then_inc(a.misc_full, 1)
                        elif e == "M":
                            wait_alone(pe, a.m_cut, s)
                            for i in range(2 * lay.kinds):
                                last = pe.transpose(misc[0:48, :].bitcast(BF)[:, P * i:P * i + P],
                                                    nmax_p[:, i, :, :, :].rearrange("p s r j -> p (s r j)"), identb[:, :])
                            last.then_inc(a.misc_full, 1)
                        elif e in ("Y0", "Y1", "Y2"):
                            k = int(e[1])
                            b = s - (2 if k == 0 else 3)
                            pe.wait_ge(a.yu_ready, b * 3 + (k + 1) if lay.own else b + 1)
                            for q in range(2):
                                for g in range(2):
                                    at = P * (2 * q + g)
                                    last = pe.transpose(misc[:, at:at + P], yu[:, T * g + P * q:T * g + P * q + P],
                                                        identf[:, :])
                            last.then_inc(a.misc_full, 1)
                        elif e == "YT":
                            if lay.own:
                                pe.wait_ge(a.y_ready, s - 2)
                            for i in range(2):
                                last = pe.transpose(misc[:, P * i:P * i + P], y_all[:, i, :], identf[:, :])
                            last.then_inc(a.misc_full, 1)
                        elif e == "O":
                            for i in range(2):
                                last = pe.matmul(misc[:, P * i:P * i + P], yt[:, P * i:P * i + P], wa[:, 4 if lay.own else 1, :],
                                                 start=True, stop=True)
                            last.then_inc(a.misc_full, 1)

                steps(pe, step)
                if l == 1:
                    break
                f, units = F, U0
                pe.wait_ge(gu0_in, 48)

                def prepare(what, c, par, used):
                    at_least(pe, f.misc_free, used)
                    if what == "XT":
                        pe.wait_ge(f.xn_ready, c + 1)
                        for i in range(CT):
                            last = pe.transpose(misc[:, P * i:P * i + P], xn_f[:, i, :], identf[:, :])
                    elif what == "R":
                        w, ne = w_router0, E0
                        for i in range(CT):
                            last = pe.matmul(misc[:, ne * i:ne * i + ne], xt_f[:, par, P * i:P * i + P], w[:, :],
                                             start=True, stop=True)
                    else:
                        pe.wait_ge(f.w_cut, c + 1)
                        n = 3 * E0
                        for i in range(CT):
                            last = pe.transpose(misc[0:n, :].bitcast(BF)[:, P * i:P * i + P], w_parts[:, i, 0:n], identb[:, :])
                    last.then_inc(f.misc_full, 1)

                def output(c, used):
                    at_least(pe, f.misc_free, used)
                    pe.wait_ge(f.yt_ready, c + 1)
                    for i in range(CT):
                        last = pe.transpose(misc[:, P * i:P * i + P], yt_f[:, P * i:P * i + P], identf[:, :])
                    last.then_inc(f.misc_full, 1)

                def spread(c, par, e):
                    at_least(pe, f.h_ready, c * units + e - 1)
                    pe.matmul(wb_ps[e % 2][:, :], sel0[:, e, :], wt_f[par], start=True, stop=True)\
                      .then_inc(f.wb_full, 1)

                def chunk(c, par, more):
                    pe.wait_ge(f.misc_free, 3 if isinstance(c, int) and c == 0 else c * 4 + 2)
                    for u in range(units + 1):
                        n = c * units + u
                        slot = (par * units + u) % 2
                        if u < units:
                            w_gate, w_up, x_up = w_gate0[:, u, :], w_up0[:, u, :], xt_f[:, par, :]
                            at_least(pe, f.s_ready, n - 1)
                            pe.matmul(gate_ps[slot][:, :], w_gate, xt_f[:, par, :], start=True, stop=True)\
                              .then_inc(f.gate_full, 1)
                            at_least(pe, f.t_ready, n - 1)
                            pe.matmul(up_ps[slot][:, :], w_up, x_up, start=True, stop=True).then_inc(f.up_full, 1)
                            if u < units - 1:
                                spread(c, par, u)
                        if u:
                            if u == 1:
                                at_least(pe, f.yt_ready, c)
                            pe.wait_ge(f.h_ready, n)
                            w_down = w_down0[:, u - 1, :]
                            pe.matmul(y_ps[:, :], w_down, hid_h[:, 1 - slot, :], start=(u == 1), stop=(u == units))\
                              .then_inc(f.h_used, 1)
                        if u == Y_AT and (not isinstance(c, int) or c):
                            output(c - 1, c * 4 + 2)
                        for what, at, use in ROUTING:
                            if at == u and more:
                                prepare(what, c + 1, 1 - par, c * 4 + use)

                for i, what in enumerate(("XT", "R", "W")):
                    prepare(what, 0, 0, i)
                chunks(pe, chunk)
                output(NCH - 1, F_USES - 1)

            pe.wait_ge(A[1].misc_free, LAYERS[1].total)
            for c in range(NCH + 1):
                if c < NCH:
                    pe.wait_ge(S.xn_ready, c + 1)
                    at_least(pe, S.xt_copied, c - 1)
                    for k in range(CT):
                        last = pe.transpose(bank[c % 2][:, P * k:P * k + P], xn_all[:, c * CT + k, :], identf[:, :])
                    last.then_inc(S.xt_full, 1)
                if c:
                    pe.wait_ge(S.xt_copied, c)
                    for k in range(CT):
                        at = ((c - 1) * CT + k) * E1
                        last = pe.matmul(bank[2][:, at:at + E1], xt_f[:, (c - 1) % 2, P * k:P * k + P], w_router1[:, :],
                                         start=True, stop=True)
                    last.then_inc(S.routed, 1)
            pe.wait_ge(S.sel_ready, 1)
            n = NT * E1
            pe.matmul(bank[3][:, 0:n], tri[:, :], sel, start=True, stop=False, skip_group_check=True)
            for d in range(1, NT):
                pe.matmul(bank[3][:, d * E1:n], ones[:, :], sel[:, 0:n - d * E1], start=False, stop=(d == NT - 1),
                          skip_group_check=True)
            pe.matmul(bank[4][:, 0:E1], ones[:, :], sel_sum, start=True, stop=True).then_inc(S.rank_ready, 1)
            pe.wait_ge(w1_in, 32)
            pe.wait_ge(S.te_ready, 1)

            def turn_x(i, q, turn):
                pe.wait_ge(S.tile_in[q], turn)
                at_least(pe, S.x_copied, i)
                pe.transpose(misc[:, 0:P], tile_x[:, q, :], identf[:, :]).then_inc(S.x_taken, 1)

            def down(i, k, e):
                pe.wait_ge(S.ht_copied, i + 1)
                at_least(pe, S.y_ready, i)
                for n in range(4):
                    last = pe.matmul(y_ps[:, 0:P], tile_ht[:, k, P * n:P * n + P],
                                     w_dn_s[:, bass.ds(e, 1), n, :].rearrange("p a n -> p (a n)"),
                                     start=(n == 0), stop=(n == 3))
                last.then_inc(S.y_full, 1)

            def turn_h(i, k):
                pe.wait_ge(S.h_ready, i + 1)
                at_least(pe, S.ht_copied, i - 1)
                for n in range(4):
                    last = pe.transpose(wb_ps[k][:, P * n:P * n + P], hid_h[:, k, P * n:P * n + P], identf[:, :])
                last.then_inc(S.ht_full, 1)

            def expert(i):
                return pe.value_load(expert_of[0:1, bass.ds(i, 1)], min_val=0, max_val=E1 - 1)

            def tile(i, q, turn, before, e, more):
                k = q % 2
                pe.wait_ge(S.x_copied, i + 1)
                at_least(pe, S.s_ready, i - 1)
                w = lambda a: w_gu_s[:, bass.ds(e, 1), a, :].rearrange("p a n -> p (a n)")
                pe.matmul(gate_ps[k][:, :], tile_xt[:, k, :], w(0), start=True, stop=True).then_inc(S.gate_full, 1)
                if before is not None:
                    turn_h(i - 1, 1 - k)
                at_least(pe, S.h_ready, i - 1)
                pe.matmul(up_ps[k][:, :], tile_xt[:, k, :], w(1), start=True, stop=True).then_inc(S.up_full, 1)
                after = expert(i + 1) if more else None
                if more:
                    turn_x(i + 1, (q + 1) % NBUF, turn)
                if before is not None:
                    down(i - 1, 1 - k, before)
                return e, after

            turn_x(0, 0, 16)
            before, e = None, expert(0)
            for i in range(NBUF):
                before, e = tile(i, i, 16 * ((i + 1) // NBUF + 1), before, e, True)
            with pe.Fori(0, (ST - 2 * NBUF) // NBUF) as g:
                before, e = expert(g * NBUF + (NBUF - 1)), expert(g * NBUF + NBUF)
                for q in range(NBUF):
                    before, e = tile(g * NBUF + (NBUF + q), q, (g + (2 if q < NBUF - 1 else 3)) * 16, before, e, True)
            before, e = expert(ST - NBUF - 1), expert(ST - NBUF)
            for i in range(ST - NBUF, ST):
                before, e = tile(i, i % NBUF, 16 * ((i + 1) // NBUF + 1), before, e, i + 1 < ST)
            turn_h(ST - 1, 1)
            down(ST - 1, 1, before)


_INS = ("c_identf", "c_identb", "c_keep", "c_mask_nat", "c_mask_tr", "c_lower", "c_sel0", "c_tri", "c_ones", "c_route", "c_tail", "c_tail_ctx", "c_zero",
        "biases", "w_att0",
        "w_att1", "w_ctx", "w_router0", "w_router1", "bp", "router_bias", "ctx", "x", "w_gate0", "w_up0", "w_down0",
        "w_gu1", "w_dn1")


def kernel(**inputs):
    import ml_dtypes as _ml
    import numpy as _np
    import concourse.bacc as _bacc
    from concourse import mybir as _mybir
    from concourse.bass_utils import run_bass_kernel_spmd as _run

    g = {k: _np.asarray(v) for k, v in inputs.items()}
    f32, bf16 = _np.float32, _ml.bfloat16
    perm = _np.array([(2 * j + s) * D + d for s in range(2) for d in range(D) for j in range(NJ)])
    heads = lambda w: w[:, perm]
    a = {}
    a["c_identf"] = _np.eye(P, dtype=f32)
    a["c_identb"] = _np.eye(P, dtype=f32).astype(bf16)
    a["c_keep"] = _np.stack([_np.arange(P) < 64, _np.arange(P) >= 64], 1).astype(f32)
    later = _np.triu(_np.full((P, P), MASKED, f32), 1)
    a["c_mask_nat"] = _np.stack([later, later], 1).astype(bf16)
    a["c_mask_tr"] = _np.stack([later.T, later.T], 1).astype(bf16)
    a["c_lower"] = _np.broadcast_to(_np.tril(_np.ones((G0, G0), f32), -1), (P, G0, G0))
    per, w = P // I0, I0
    pick = _np.zeros((P, E0 // per, P), f32)
    for r in range(3):
        for e in range(E0):
            pick[r * E0 + e, e // per, (e % per) * w:(e % per) * w + w] = 1
    a["c_sel0"] = pick.astype(bf16)
    tail = _np.zeros((P - SROWS, 2, T), f32)
    tail[0:3, 0], tail[3:6, 1] = 1, 1
    a["c_tail"] = tail.reshape(P - SROWS, 2 * T).astype(bf16)
    a["c_tail_ctx"] = tail[:, :, 0:TC].reshape(P - SROWS, 2 * TC).astype(bf16)
    a["c_zero"] = _np.zeros((P - SROWS, NJ * 2 * T), f32).astype(bf16)
    a["c_tri"] = _np.triu(_np.ones((P, P), f32), 1).astype(bf16)
    a["c_ones"] = _np.ones((P, P), f32).astype(bf16)
    row = _np.concatenate([E1 - _np.arange(E1), P * _np.arange(NT), _np.tril(_np.ones((E1, E1))).ravel(), _np.arange(ST)])
    a["c_route"] = _np.broadcast_to(row.astype(f32), (P, row.size))
    a["biases"] = _np.stack([g["L0_xattn_bq"][perm], g["L0_xattn_bcq"][perm], g["L0_xattn_bk"][perm],
                             g["L0_xattn_bck"][perm], g["L0_xattn_bv"], g["L0_xattn_bcv"]], 1)
    a["w_att0"] = _np.stack([heads(g["L0_xattn_Wq"]), heads(g["L0_xattn_Wcq"]), heads(g["L0_xattn_Wk"]),
                             g["L0_xattn_Wv"], g["L0_xattn_Wp"]], 1)
    a["w_att1"] = _np.stack([heads(g["L1_xattn_Wq"].T), g["L1_xattn_Wo"].T], 1)
    kv1 = g["L1_xattn_Wkv"].T
    a["w_ctx"] = _np.stack([_np.stack([heads(g["L0_xattn_Wck"]), g["L0_xattn_Wcv"]], 1),
                            _np.stack([heads(kv1[:, 0:C]), kv1[:, C:2 * C]], 1)], 1)
    a["w_router0"], a["w_router1"] = g["L0_ffn_router_weight"].T, g["L1_ffn_gate_w"].T
    a["bp"], a["router_bias"] = g["L0_xattn_bp"], g["L0_ffn_router_bias"]
    a["ctx"] = g["ctx_512"].reshape(NCTX, CC).T
    a["x"] = g["x"].reshape(NT, P, C).transpose(1, 0, 2)
    units = lambda w, s: _np.concatenate([w.reshape(E0 * I0, C), s]).T.reshape(C, U0, P)
    a["w_gate0"] = units(g["L0_ffn_gate_w"], g["L0_ffn_shared_gate_w"])
    a["w_up0"] = units(g["L0_ffn_up_w"], g["L0_ffn_shared_up_w"])
    down = _np.concatenate([g["L0_ffn_down_w"].transpose(0, 2, 1).reshape(E0 * I0, C), g["L0_ffn_shared_down_w"].T])
    a["w_down0"] = down.reshape(U0, P, C).transpose(1, 0, 2)
    a["w_gu1"] = g["L1_ffn_gate_up_proj"].reshape(E1, 2, I1, C).transpose(3, 0, 1, 2)
    a["w_dn1"] = g["L1_ffn_down_proj"].transpose(0, 2, 1).reshape(E1, 4, P, C).transpose(2, 0, 1, 3)

    nc = _bacc.Bacc("TRN2", target_bir_lowering=False, num_devices=1)
    arrays, aps = {}, {}
    for name in _INS:
        v = _np.ascontiguousarray(a[name])
        arrays[f"in_{name}"] = v
        aps[name] = nc.dram_tensor(f"in_{name}", v.shape, _mybir.dt.from_np(v.dtype), kind="ExternalInput").ap()
    out = nc.dram_tensor("out_0", (P, NT, C), _mybir.dt.float32, kind="ExternalOutput").ap()
    bass_two_layers(nc, aps, out)
    r = _run(nc, [arrays], core_ids=[0])
    got = r.results[0]["out_0"]
    return got.transpose(1, 0, 2).reshape(B, T, C)
```
